# Optimizing a Trainium2 kernel written in Bass

```python
import numpy as np
import jax
import jax.numpy as jnp

def _softmax(x, axis=-1):
    return jax.nn.softmax(x, axis=axis)

def _gelu(x):
    return jax.nn.gelu(x, approximate=True)

def _silu(x):
    return jax.nn.silu(x)

def _sigmoid(x):
    return jax.nn.sigmoid(x)

def _layernorm(x, axis=-1, eps=1e-05):
    m = jnp.mean(x, axis=axis, keepdims=True)
    v = jnp.var(x, axis=axis, keepdims=True)
    return (x - m) / jnp.sqrt(v + eps)

def _scatter_add(tgt, idx, src, axis=0):
    return tgt.at[idx].add(src)

def _segment_sum(src, seg, n):
    return jax.ops.segment_sum(src, seg, n)
kernel_name = 'mk_dlrm_tower_d1_rec_r8_6e79da'

def setup_inputs(seed: int=0):
    np.random.seed(seed)
    _w = jnp.asarray

    def _rec_inputs():
        import jax
        import jax.numpy as jnp
        _tk = jax.random.key(seed)
        ids = jnp.stack([jax.random.randint(jax.random.fold_in(_tk, 200 + f), (2048,), 0, v, jnp.int32) for f, v in enumerate([125000, 1000, 12500, 1000, 125000, 12500, 125000, 1250, 12500, 1250, 12500, 1000, 12500, 1250, 12500, 12500, 1000, 12500, 1000, 1000, 1000, 1250, 1000, 1250, 1000, 1250])], axis=1)
        tbl_0 = 0.05 * jax.random.normal(jax.random.fold_in(_tk, 500 + 0), (125000, 64), jnp.float32)
        tbl_1 = 0.05 * jax.random.normal(jax.random.fold_in(_tk, 500 + 1), (1000, 64), jnp.float32)
        tbl_2 = 0.05 * jax.random.normal(jax.random.fold_in(_tk, 500 + 2), (12500, 64), jnp.float32)
        tbl_3 = 0.05 * jax.random.normal(jax.random.fold_in(_tk, 500 + 3), (1000, 64), jnp.float32)
        tbl_4 = 0.05 * jax.random.normal(jax.random.fold_in(_tk, 500 + 4), (125000, 64), jnp.float32)
        tbl_5 = 0.05 * jax.random.normal(jax.random.fold_in(_tk, 500 + 5), (12500, 64), jnp.float32)
        tbl_6 = 0.05 * jax.random.normal(jax.random.fold_in(_tk, 500 + 6), (125000, 64), jnp.float32)
        tbl_7 = 0.05 * jax.random.normal(jax.random.fold_in(_tk, 500 + 7), (1250, 64), jnp.float32)
        tbl_8 = 0.05 * jax.random.normal(jax.random.fold_in(_tk, 500 + 8), (12500, 64), jnp.float32)
        tbl_9 = 0.05 * jax.random.normal(jax.random.fold_in(_tk, 500 + 9), (1250, 64), jnp.float32)
        tbl_10 = 0.05 * jax.random.normal(jax.random.fold_in(_tk, 500 + 10), (12500, 64), jnp.float32)
        tbl_11 = 0.05 * jax.random.normal(jax.random.fold_in(_tk, 500 + 11), (1000, 64), jnp.float32)
        tbl_12 = 0.05 * jax.random.normal(jax.random.fold_in(_tk, 500 + 12), (12500, 64), jnp.float32)
        tbl_13 = 0.05 * jax.random.normal(jax.random.fold_in(_tk, 500 + 13), (1250, 64), jnp.float32)
        tbl_14 = 0.05 * jax.random.normal(jax.random.fold_in(_tk, 500 + 14), (12500, 64), jnp.float32)
        tbl_15 = 0.05 * jax.random.normal(jax.random.fold_in(_tk, 500 + 15), (12500, 64), jnp.float32)
        tbl_16 = 0.05 * jax.random.normal(jax.random.fold_in(_tk, 500 + 16), (1000, 64), jnp.float32)
        tbl_17 = 0.05 * jax.random.normal(jax.random.fold_in(_tk, 500 + 17), (12500, 64), jnp.float32)
        tbl_18 = 0.05 * jax.random.normal(jax.random.fold_in(_tk, 500 + 18), (1000, 64), jnp.float32)
        tbl_19 = 0.05 * jax.random.normal(jax.random.fold_in(_tk, 500 + 19), (1000, 64), jnp.float32)
        tbl_20 = 0.05 * jax.random.normal(jax.random.fold_in(_tk, 500 + 20), (1000, 64), jnp.float32)
        tbl_21 = 0.05 * jax.random.normal(jax.random.fold_in(_tk, 500 + 21), (1250, 64), jnp.float32)
        tbl_22 = 0.05 * jax.random.normal(jax.random.fold_in(_tk, 500 + 22), (1000, 64), jnp.float32)
        tbl_23 = 0.05 * jax.random.normal(jax.random.fold_in(_tk, 500 + 23), (1250, 64), jnp.float32)
        tbl_24 = 0.05 * jax.random.normal(jax.random.fold_in(_tk, 500 + 24), (1000, 64), jnp.float32)
        tbl_25 = 0.05 * jax.random.normal(jax.random.fold_in(_tk, 500 + 25), (1250, 64), jnp.float32)
        _rk = jax.random.fold_in(_tk, 7)
        r_dense_t = 7.22013e-05 + 1.00017 * jax.random.normal(jax.random.fold_in(_rk, 101), (2048, 256), jnp.float32)
        W_top1 = 0.0360844 * jax.random.normal(jax.random.fold_in(_tk, 801), (768, 512), jnp.float32)
        W_top2 = 0.0441942 * jax.random.normal(jax.random.fold_in(_tk, 802), (512, 256), jnp.float32)
        W_top3 = 0.0625 * jax.random.normal(jax.random.fold_in(_tk, 803), (256, 1), jnp.float32)
        b_top1 = jnp.zeros((512,), jnp.float32)
        b_top2 = jnp.zeros((256,), jnp.float32)
        return (r_dense_t, ids, tbl_0, tbl_1, tbl_2, tbl_3, tbl_4, tbl_5, tbl_6, tbl_7, tbl_8, tbl_9, tbl_10, tbl_11, tbl_12, tbl_13, tbl_14, tbl_15, tbl_16, tbl_17, tbl_18, tbl_19, tbl_20, tbl_21, tbl_22, tbl_23, tbl_24, tbl_25, W_top1, b_top1, W_top2, b_top2, W_top3)
    r_dense_t, ids, tbl_0, tbl_1, tbl_2, tbl_3, tbl_4, tbl_5, tbl_6, tbl_7, tbl_8, tbl_9, tbl_10, tbl_11, tbl_12, tbl_13, tbl_14, tbl_15, tbl_16, tbl_17, tbl_18, tbl_19, tbl_20, tbl_21, tbl_22, tbl_23, tbl_24, tbl_25, W_top1, b_top1, W_top2, b_top2, W_top3 = _rec_inputs()

    def _L0_rec_setup():
        import jax, jax.numpy as jnp
        import numpy as np
        EPS = 1e-05
        NI = 33
        TRIL_I, TRIL_J = np.tril_indices(NI, k=-1)

        def layer_norm(x, g, b):
            m = jnp.mean(x, axis=-1, keepdims=True)
            v = jnp.mean(jnp.square(x - m), axis=-1, keepdims=True)
            return (x - m) * jax.lax.rsqrt(v + EPS) * g + b
        key = jax.random.key(seed)
        ks = jax.random.split(key, 8)
        B, D_DENSE, N_SP, D_SP = (4096, 256, 26, 64)
        E, PROJ, MAXD, NFLAT = (128, 32, 512, 528)
        dense_t = jax.random.normal(ks[0], (B, D_DENSE), dtype=jnp.float32)
        sparse_t = jax.random.normal(ks[1], (B, N_SP, D_SP), dtype=jnp.float32)
        Wd = jax.random.normal(ks[2], (E, D_DENSE), dtype=jnp.float32) / np.sqrt(D_DENSE)
        Ws = jax.random.normal(ks[3], (E, D_SP), dtype=jnp.float32) / np.sqrt(D_SP)
        Wsi = jax.random.normal(ks[4], (PROJ, N_SP), dtype=jnp.float32) / np.sqrt(N_SP)
        Wl = jax.random.normal(ks[5], (MAXD, NFLAT), dtype=jnp.float32) / np.sqrt(NFLAT)
        gd = jnp.ones((E,), jnp.float32)
        bd = jnp.zeros((E,), jnp.float32)
        gs = jnp.ones((E,), jnp.float32)
        bs = jnp.zeros((E,), jnp.float32)
        gsi = jnp.ones((PROJ,), jnp.float32)
        bsi = jnp.zeros((PROJ,), jnp.float32)
        gl = jnp.ones((MAXD,), jnp.float32)
        bl = jnp.zeros((MAXD,), jnp.float32)
        return {'dense_t': dense_t, 'sparse_t': sparse_t, 'Wd': Wd, 'gd': gd, 'bd': bd, 'Ws': Ws, 'gs': gs, 'bs': bs, 'Wsi': Wsi, 'gsi': gsi, 'bsi': bsi, 'Wl': Wl, 'gl': gl, 'bl': bl, 'dims_in_use': 384}
    _L0_rec_all = _L0_rec_setup()
    _L0_rec_in = {k: v for k, v in _L0_rec_all.items() if k in ('Wd', 'gd', 'bd', 'Ws', 'gs', 'bs', 'Wsi', 'gsi', 'bsi', 'Wl', 'gl', 'bl')}
    del _L0_rec_all
    return {'r_dense_t': r_dense_t, 'ids': ids, 'tbl_0': tbl_0, 'tbl_1': tbl_1, 'tbl_2': tbl_2, 'tbl_3': tbl_3, 'tbl_4': tbl_4, 'tbl_5': tbl_5, 'tbl_6': tbl_6, 'tbl_7': tbl_7, 'tbl_8': tbl_8, 'tbl_9': tbl_9, 'tbl_10': tbl_10, 'tbl_11': tbl_11, 'tbl_12': tbl_12, 'tbl_13': tbl_13, 'tbl_14': tbl_14, 'tbl_15': tbl_15, 'tbl_16': tbl_16, 'tbl_17': tbl_17, 'tbl_18': tbl_18, 'tbl_19': tbl_19, 'tbl_20': tbl_20, 'tbl_21': tbl_21, 'tbl_22': tbl_22, 'tbl_23': tbl_23, 'tbl_24': tbl_24, 'tbl_25': tbl_25, 'W_top1': W_top1, 'b_top1': b_top1, 'W_top2': W_top2, 'b_top2': b_top2, 'W_top3': W_top3, 'L0_rec_Wd': _L0_rec_in['Wd'], 'L0_rec_gd': _L0_rec_in['gd'], 'L0_rec_bd': _L0_rec_in['bd'], 'L0_rec_Ws': _L0_rec_in['Ws'], 'L0_rec_gs': _L0_rec_in['gs'], 'L0_rec_bs': _L0_rec_in['bs'], 'L0_rec_Wsi': _L0_rec_in['Wsi'], 'L0_rec_gsi': _L0_rec_in['gsi'], 'L0_rec_bsi': _L0_rec_in['bsi'], 'L0_rec_Wl': _L0_rec_in['Wl'], 'L0_rec_gl': _L0_rec_in['gl'], 'L0_rec_bl': _L0_rec_in['bl']}

def reference(r_dense_t, ids, tbl_0, tbl_1, tbl_2, tbl_3, tbl_4, tbl_5, tbl_6, tbl_7, tbl_8, tbl_9, tbl_10, tbl_11, tbl_12, tbl_13, tbl_14, tbl_15, tbl_16, tbl_17, tbl_18, tbl_19, tbl_20, tbl_21, tbl_22, tbl_23, tbl_24, tbl_25, W_top1, b_top1, W_top2, b_top2, W_top3, L0_rec_Wd, L0_rec_gd, L0_rec_bd, L0_rec_Ws, L0_rec_gs, L0_rec_bs, L0_rec_Wsi, L0_rec_gsi, L0_rec_bsi, L0_rec_Wl, L0_rec_gl, L0_rec_bl):
    import jax
    import jax.numpy as jnp

    def _L0_rec_ref(dense_t, sparse_t, Wd, gd, bd, Ws, gs, bs, Wsi, gsi, bsi, Wl, gl, bl, dims_in_use):
        import jax, jax.numpy as jnp
        import numpy as np
        EPS = 1e-05
        NI = 33
        TRIL_I, TRIL_J = np.tril_indices(NI, k=-1)

        def layer_norm(x, g, b):
            m = jnp.mean(x, axis=-1, keepdims=True)
            v = jnp.mean(jnp.square(x - m), axis=-1, keepdims=True)
            return (x - m) * jax.lax.rsqrt(v + EPS) * g + b
        x = layer_norm(dense_t @ Wd.T, gd, bd)
        y = layer_norm(jnp.einsum('bnd,ed->bne', sparse_t, Ws), gs, bs)
        y = jnp.einsum('bne,pn->bep', y, Wsi)
        y = layer_norm(y, gsi, bsi)
        y = jnp.swapaxes(y, 1, 2)
        T = jnp.concatenate([x[:, None, :], y], axis=1)
        Z = jnp.einsum('bnd,bmd->bnm', T, T)
        Zflat = Z[:, TRIL_I, TRIL_J]
        out = layer_norm(Zflat @ Wl.T, gl, bl)
        maxd = out.shape[-1]
        mask = (jnp.arange(maxd) < dims_in_use).astype(out.dtype)
        return out * mask
    e = jnp.stack([tbl_0[ids[:, 0]], tbl_1[ids[:, 1]], tbl_2[ids[:, 2]], tbl_3[ids[:, 3]], tbl_4[ids[:, 4]], tbl_5[ids[:, 5]], tbl_6[ids[:, 6]], tbl_7[ids[:, 7]], tbl_8[ids[:, 8]], tbl_9[ids[:, 9]], tbl_10[ids[:, 10]], tbl_11[ids[:, 11]], tbl_12[ids[:, 12]], tbl_13[ids[:, 13]], tbl_14[ids[:, 14]], tbl_15[ids[:, 15]], tbl_16[ids[:, 16]], tbl_17[ids[:, 17]], tbl_18[ids[:, 18]], tbl_19[ids[:, 19]], tbl_20[ids[:, 20]], tbl_21[ids[:, 21]], tbl_22[ids[:, 22]], tbl_23[ids[:, 23]], tbl_24[ids[:, 24]], tbl_25[ids[:, 25]]], axis=1)
    z = _L0_rec_ref(r_dense_t, e, L0_rec_Wd, L0_rec_gd, L0_rec_bd, L0_rec_Ws, L0_rec_gs, L0_rec_bs, L0_rec_Wsi, L0_rec_gsi, L0_rec_bsi, L0_rec_Wl, L0_rec_gl, L0_rec_bl, 384)
    z = z.reshape(z.shape[0], -1)
    h = jnp.concatenate([z, r_dense_t], axis=1)
    h = jnp.maximum(h @ W_top1 + b_top1, 0.0)
    h = jnp.maximum(h @ W_top2 + b_top2, 0.0)
    y = h @ W_top3
    return y

_drawn_inputs = setup_inputs


def setup_inputs(seed=0):
    import zlib

    import numpy as np

    out = dict(_drawn_inputs(seed))
    spreads = {'b_top1': (0.0, 0.1),
     'b_top2': (0.0, 0.1),
     'L0_rec_gd': (1.0, 0.6),
     'L0_rec_bd': (0.0, 0.8),
     'L0_rec_gs': (1.0, 0.6),
     'L0_rec_bs': (0.0, 0.1),
     'L0_rec_gsi': (1.0, 0.2),
     'L0_rec_bsi': (0.0, 0.1),
     'L0_rec_gl': (1.0, 0.2),
     'L0_rec_bl': (0.0, 0.1)}
    factors = {}
    for name, (base, spread) in spreads.items():
        noise = np.random.default_rng([zlib.crc32(name.encode()), seed]).standard_normal(out[name].shape)
        drawn = base * np.exp(spread * noise) if base else spread * noise
        out[name] = jnp.asarray(drawn.astype(out[name].dtype))
    for name, factor in factors.items():
        out[name] = (out[name] * factor).astype(out[name].dtype)
    return out
```

```python
from contextlib import ExitStack

import concourse.bass as bass
from concourse import mybir

F32 = mybir.dt.float32
I32 = mybir.dt.int32
ALU = mybir.AluOpType
ACT = mybir.ActivationFunctionType
AX = mybir.AxisListType

ROWS = 2048
NTAB, D = 26, 64
E_DIM, PROJ = 128, 32
D_DENSE = 256
MAXD, USED = 512, 384
H1, H2 = 512, 256
NPAIR = (PROJ + 1) * PROJ // 2
EPS = 1e-5
P = 128

TILE = 128
NTILE = ROWS // TILE
UNIT = 32
UPT = TILE // UNIT
SUPER = 512
TPS = SUPER // TILE
NSUPER = ROWS // SUPER
BPG = 4
GROWS = BPG * NTAB
GPU = UNIT // BPG
GPS = SUPER // BPG
UPS = TPS * UPT
LEAD = 6

PAIRS = [4, 3, 3, 3]
TAB0 = [0, 8, 14, 20, 26]
QN = PROJ + 2

BLOCKS = [(0, 0, 16, 16, 16)]
BLOCKS += [(256 + 64 * h, 16 * h, 8, 16 * h + 8, 8) for h in range(2)]
BLOCKS += [(384 + 64 * t, 8 * t, 8, 8 * t, 8) for t in range(4)]
NFULL = 5
LASTK = 2 * PROJ + 1
WRITES = BPG * (len(BLOCKS) + 1)
READS = NFULL + 1


def interaction_tower(nc, a, out):
    tables = [a[f"tbl_{n}"] for n in range(NTAB)]
    scaled_d = nc.dram_tensor("scaled_d", (NTILE, TILE * NTAB, D), F32, kind="Internal").ap()
    gram_d = nc.dram_tensor("gram_d", (NSUPER, NFULL * P + 2 * PROJ, BPG, GPS), F32, kind="Internal").ap()

    with ExitStack() as ctx:
        ctx.enter_context(nc.allow_non_contiguous_dma(reason="bias vectors, once"))

        def sb(name, shape, dt=F32):
            return ctx.enter_context(nc.sbuf_tensor(name, shape, dt))

        def pb(name, shape):
            return ctx.enter_context(nc.psum_tensor(name, shape, F32))

        def sem(name):
            return ctx.enter_context(nc.semaphore(name))

        ps_tr = pb("ps_tr", [P, 512])
        ps_gm = pb("ps_gm", [P, 512])
        ps_q = pb("ps_q", [P, 512])
        ps_y = pb("ps_y", [P, 2, 512])
        ps_rf = pb("ps_r", [P, 512])
        ps_r = ps_rf[:, 0:GPU * QN].rearrange("p (g q) -> p g q", q=QN)
        ps_ab = [pb("ps_a", [P, 512]), pb("ps_b", [P, 512])]

        ident = sb("ident", [P, P])
        ones = sb("ones", [P, P])
        mean_e = sb("mean_e", [P, P])
        mean_o = sb("mean_o", [P, P])
        mean_p = sb("mean_p", [PROJ, PROJ])
        group_mask = sb("group_mask", [GROWS, BPG])

        ws = sb("ws", [P, D])
        wd = sb("wd", [P, D_DENSE])
        wsi = sb("wsi", [PROJ, NTAB])
        vec = sb("vec", [P, 4])
        gsi_row = sb("gsi_row", [1, 2 * PROJ])
        w1 = sb("w1", [P, 5, H1])
        w2 = sb("w2", [P, 4, H2])
        w3 = sb("w3", [P, 2])
        b1 = sb("b1", [P, 4])
        b2 = sb("b2", [P, 2])
        gl = sb("gl", [P, 3])
        bl = sb("bl", [P, 3])
        wl = sb("wl", [P, 4, NPAIR])

        wc2 = sb("wc2", [P, 2 * D])
        wg2 = sb("wg2", [P, 2 * D])
        gbd = sb("gbd", [P, P])
        wp = [sb("wp0", [P, E_DIM]), sb("wp1", [P, E_DIM])]
        wsc = sb("wsc", [PROJ, BPG, NTAB])
        wsct = sb("wsct", [GROWS, PROJ])
        wbd = sb("wbd", [GROWS, BPG, PROJ])
        bias_y = sb("bias_y", [P, PROJ])
        wdt = sb("wdt", [P, 2, E_DIM])
        gb = sb("gb", [P, 2 * PROJ])
        wl_low = sb("wl_low", [P, 4, PROJ + 1, PROJ])
        wl_x = sb("wl_x", [P, 4, NFULL * P + LASTK])
        wl_t = sb("wl_t", [P, READS, MAXD])
        const_z = sb("const_z", [P, 4])
        b1x = sb("b1x", [P, 4])
        small = sb("small", [P, 4, PROJ + 1])

        ids = sb("ids", [P, NTILE, NTAB], I32)
        idx = [sb(f"idx{i}", [P, NTAB], I32) for i in range(2)]
        emb = [sb(f"emb{i}", [P, NTAB * D]) for i in range(2)]
        emb_t = [sb(f"emb_t{i}", [P, 512]) for i in range(2)]
        prod = [sb(f"prod{i}", [P, 512]) for i in range(2)]
        var_b = sb("var_b", [P, NTAB])
        var_e = sb("var_e", [P, NTAB])
        var_r = sb("var_r", [P, NTAB])
        rs_b = sb("rs_b", [P, NTAB])
        xe = [sb(f"xe{u}", [GROWS, GPU * D]) for u in range(UPT)]
        qt = [sb(f"qt{i}", [P, 512]) for i in range(2)]
        cen = [sb(f"cen{i}", [P, 2, 4, BPG, PROJ]) for i in range(2)]
        sq = sb("sq", [P, 2, 4, BPG, PROJ])
        mov = [sb(f"mov{i}", [P, 2, 4, BPG, QN]) for i in range(2)]
        v2 = sb("v2", [P, UNIT])
        v2e = sb("v2e", [P, UNIT])
        r2 = sb("r2", [P, 2, 4, BPG])
        gram = sb("gram", [P, QN, 2 * GPS])
        f_sb = sb("f_sb", [P, NFULL, SUPER])
        f_last = sb("f_last", [LASTK, NSUPER, SUPER])
        dense_t = sb("dense_t", [P, 2, NSUPER, SUPER])
        xt = sb("xt", [P, NSUPER, SUPER])
        prep_tmp = sb("prep_tmp", [P, PROJ + 1, PROJ])

        ring = gram[:].rearrange("p q g -> p (q g)")
        dense = ring[:, 0:NTILE * D_DENSE].rearrange("p (t k) -> p t k", t=NTILE)
        x_sq = ring[:, 2 * ROWS:3 * ROWS].rearrange("p (s b) -> p s b", s=NSUPER)
        x_rs = ring[:, 3 * ROWS:4 * ROWS].rearrange("p (s b) -> p s b", s=NSUPER)
        x_rr = x_sq
        low = wl_low[:].rearrange("p c q k -> p (c q k)")
        z_c = low[:, 0:1536].rearrange("p (c b) -> p c b", c=3)
        z_sq = [low[:, 1536:2048], low[:, 2048:2560]]
        rz_v = low[:, 2560:3072]
        rz_sb = low[:, 3072:3584]
        old_wl = wl[:].rearrange("p c k -> p (c k)")
        z_sb = old_wl[:, 0:1536].rearrange("p (c b) -> p c b", c=3)
        y_sb = old_wl[0:1, 1536:2048]
        h1_sb = wl_x[:].rearrange("p c k -> p (c k)")[:, 0:4 * SUPER].rearrange("p (c b) -> p c b", c=4)
        h2_sb = prep_tmp[:].rearrange("p q k -> p (q k)")[:, 0:2 * SUPER].rearrange("p (c b) -> p c b", c=2)

        s_const = sem("const_ready")
        s_ld = {n: sem(f"ld_{n}") for n in ("ws", "wd", "wsi", "vec", "gsi", "w1", "w2", "w3", "b1", "b2",
                                            "gl", "bl", "wl", "dense")}
        s_ids = sem("ids_loaded")
        s_idx = sem("tile_ids_ready")
        s_begun = sem("gather_tiles_begun")
        s_gat = [[sem(f"gathered{i}_{u}") for u in range(4)] for i in range(2)]
        s_sw = [sem(f"scaled_written{i}") for i in range(2)]
        s_xl = [sem(f"unit_loaded{u}") for u in range(UPT)]
        s_fw = sem("gram_written")
        s_fr = sem("gram_read_back")
        s_out = sem("out_written")
        s_p = {n: sem(f"prep_p_{n}") for n in ("wsmean", "wsimean", "wdmean", "g", "wsit", "wdt", "wpt", "sc",
                                               "dense_t", "x", "xvar", "wlmean", "gb", "sx", "wlt", "b1")}
        s_a = {n: sem(f"prep_a_{n}") for n in ("wdt", "dense_t", "xsq", "xrs", "sx", "wlt")}
        s_v = {n: sem(f"prep_v_{n}") for n in ("wc", "wsi", "wd", "g", "wsct", "wbd", "wp", "bias", "xc", "xvar",
                                               "xrr", "x", "wlsub", "gb", "wlrows", "b1")}
        s_tr = sem("emb_transposed")
        s_gm = sem("emb_g_ready")
        s_q = sem("q_ready")
        s_y = sem("y_ready")
        s_gr = sem("gram_ready")
        s_z = sem("z_ready")
        s_ss = sem("z_square_sum_ready")
        s_h1 = sem("h1_ready")
        s_h2 = sem("h2_ready")
        s_yo = sem("y_out_ready")
        s_et = sem("emb_t_copied")
        s_qt = sem("qt_copied")
        s_sq = sem("squared")
        s_rs = sem("r_ready")
        s_g2 = sem("gram_copied")
        s_rb = sem("emb_r_ready")
        s_zc = sem("z_copied")
        s_rz = sem("z_r_ready")
        s_h1r = sem("h1_relu")
        s_h2r = sem("h2_relu")
        s_yc = sem("y_copied")
        s_chain = sem("prep_chain")
        s_gmr = sem("emb_product_ready")
        s_vb = sem("emb_var_part")
        s_vbe = sem("emb_var_eps")
        s_vbr = sem("emb_var_reciprocal")
        s_sc = sem("emb_scaled")
        s_c = sem("centred_ready")
        s_v2 = sem("feature_var")
        s_v2e = sem("feature_var_eps")
        s_r2 = sem("feature_r2")
        s_m = sem("moving_ready")
        s_zv = sem("z_var_eps")
        s_zr = sem("z_var_reciprocal")
        s_zs = sem("z_scaled")

        def steps(tile, first_unit=0, last_unit=UPT):
            return range(UPT * tile + first_unit, UPT * tile + last_unit)

        def has_front(T, k):
            return not isinstance(T, int) or UPS * T + k + LEAD < NTILE * UPT

        x_banks = [ps_y[:, 0, :], ps_y[:, 1, :], ps_ab[0][:], ps_ab[1][:]]
        var_banks = [ps_tr[:], ps_gm[:], ps_q[:], ps_rf[:]]

        block = ctx.enter_context(nc.Block())

        @block.sync
        def _(sp):
            def load(dst, src, name):
                sp.dma_start(dst, src).then_inc(s_ld[name], 16)

            def write_scaled(tile, parity):
                sp.wait_ge(s_sc, tile + 1)
                sp.dma_start(scaled_d[tile].rearrange("(b n) d -> b (n d)", n=NTAB),
                             emb[parity][:]).then_inc(s_sw[parity], 16)

            def load_unit(tile, parity, nth, u, first):
                if u == 0:
                    sp.wait_ge(s_sw[parity], 16 * nth)
                if not first:
                    sp.wait_ge(s_q, tile * UPT + (u - UPT + 1))
                src = scaled_d[tile][u * GPU * GROWS:(u + 1) * GPU * GROWS, :].rearrange(
                    "(g r) d -> r g d", r=GROWS)
                sp.dma_start(xe[u][:].rearrange("r (g d) -> r g d", g=GPU), src).then_inc(s_xl[u], 16)

            def write_gram(S):
                sp.wait_ge(s_g2, UPS * S + UPS)
                g0 = (S * GPS) % (2 * GPS)
                for j in range(BPG):
                    for row, q0, nq, p0, np_ in BLOCKS:
                        sp.dma_start(
                            gram_d[S][row:row + nq * np_, j, :].rearrange("(q p) g -> p q g", q=nq),
                            gram[PROJ * j + p0:PROJ * j + p0 + np_, q0:q0 + nq, bass.ds(g0, GPS)],
                        ).then_inc(s_fw, 16)
                    sp.dma_start(
                        gram_d[S][NFULL * P:, j, :].rearrange("(q p) g -> p q g", q=2),
                        gram[PROJ * j:PROJ * (j + 1), PROJ:QN, bass.ds(g0, GPS)],
                    ).then_inc(s_fw, 16)

            def read_gram(S):
                sp.wait_ge(s_zv, S + 1)
                sp.wait_ge(s_fw, 16 * WRITES * (S + 2))
                for c in range(NFULL):
                    sp.dma_start(f_sb[:, c, :], gram_d[S][c * P:(c + 1) * P].rearrange("r j g -> r (j g)")
                                 ).then_inc(s_fr, 16)
                sp.dma_start(f_last[0:2 * PROJ, S, :], gram_d[S][NFULL * P:].rearrange("r j g -> r (j g)")
                             ).then_inc(s_fr, 16)

            def tile_step(T, c, last=False):
                tile = TPS * T + c
                if not last:
                    nxt = tile + 1
                    write_scaled(nxt, (c + 1) % 2)
                    for u in range(UPT - 1):
                        load_unit(nxt, (c + 1) % 2, 2 * T + (c + 1) // 2 + 1, u, False)
                if c == TPS:
                    write_gram(T)
                if not last:
                    load_unit(nxt, (c + 1) % 2, 2 * T + (c + 1) // 2 + 1, UPT - 1, False)
                if c == TPS:
                    read_gram(T)

            sp.sem_inc(s_fw, 16 * WRITES)
            sp.dma_start(ids[:], a["ids"].rearrange("(t p) n -> p t n", p=TILE)).then_inc(s_ids, 16)
            load(ws[:], a["L0_rec_Ws"], "ws")
            for n, v in enumerate(("gs", "bs", "gd", "bd")):
                load(vec[:, n:n + 1], a[f"L0_rec_{v}"].rearrange("(e o) -> e o", o=1), "vec")
            load(wsi[:], a["L0_rec_Wsi"], "wsi")
            load(wd[:], a["L0_rec_Wd"], "wd")
            load(dense, a["r_dense_t"].rearrange("(t p) k -> p t k", p=TILE), "dense")
            load(gsi_row[:, 0:PROJ], a["L0_rec_gsi"].rearrange("(o p) -> o p", o=1), "gsi")
            load(gsi_row[:, PROJ:], a["L0_rec_bsi"].rearrange("(o p) -> o p", o=1), "gsi")
            load(wl[:], a["L0_rec_Wl"].rearrange("(c o) k -> o c k", o=P), "wl")
            load(w1[:, 0:3, :], a["W_top1"][0:USED, :].rearrange("(c k) h -> k c h", k=P), "w1")
            load(w1[:, 3:5, :], a["W_top1"][MAXD:, :].rearrange("(c k) h -> k c h", k=P), "w1")
            load(bl[:], a["L0_rec_bl"][0:USED].rearrange("(c o) -> o c", o=P), "bl")
            load(gl[:], a["L0_rec_gl"][0:USED].rearrange("(c o) -> o c", o=P), "gl")
            load(b1[:], a["b_top1"].rearrange("(c o) -> o c", o=P), "b1")
            load(w2[:], a["W_top2"].rearrange("(c k) h -> k c h", k=P), "w2")
            load(b2[:], a["b_top2"].rearrange("(c o) -> o c", o=P), "b2")
            load(w3[:], a["W_top3"].rearrange("(c k) o -> k (c o)", k=P), "w3")

            write_scaled(0, 0)
            for u in range(UPT):
                load_unit(0, 0, 1, u, True)
            tile_step(0, 0)
            tile_step(0, 1)
            with sp.Fori(0, NSUPER - 1) as T:
                for c in range(2, 6):
                    tile_step(T, c)
            tile_step(NSUPER - 1, 2)
            tile_step(NSUPER - 1, 3, last=True)
            write_gram(NSUPER - 1)
            read_gram(NSUPER - 1)

        @block.gpsimd
        def _(pool):
            nc.gpsimd.memset(ident[:], 0.0).then_inc(s_const, 1)
            nc.gpsimd.memset(group_mask[:], 1.0).then_inc(s_const, 1)
            nc.gpsimd.memset(ones[:], 1.0).then_inc(s_const, 1)
            nc.gpsimd.memset(mean_e[:], 1.0 / E_DIM).then_inc(s_const, 1)
            nc.gpsimd.memset(mean_o[:], 1.0 / MAXD).then_inc(s_const, 1)
            nc.gpsimd.memset(mean_p[:], 1.0 / PROJ).then_inc(s_const, 1)
            nc.gpsimd.memset(gbd[:], 0.0).then_inc(s_const, 1)
            nc.gpsimd.memset(wp[0][:], 0.0).then_inc(s_const, 1)
            nc.gpsimd.memset(wp[1][:], 0.0).then_inc(s_const, 1)
            pool.wait_ge(s_const, 9)
            nc.gpsimd.affine_select(out=ident[:], in_=ident[:], compare_op=ALU.not_equal, fill=1.0, base=0,
                                    pattern=[[-1, P]], channel_multiplier=1).then_inc(s_const, 1)
            nc.gpsimd.affine_select(out=group_mask[:], in_=group_mask[:], compare_op=ALU.is_ge, fill=0.0, base=0,
                                    pattern=[[-NTAB, BPG]], channel_multiplier=1).then_inc(s_const, 1)
            pool.wait_ge(s_const, 11)
            nc.gpsimd.affine_select(out=group_mask[:], in_=group_mask[:], compare_op=ALU.is_ge, fill=0.0,
                                    base=NTAB - 1, pattern=[[NTAB, BPG]], channel_multiplier=-1
                                    ).then_inc(s_const, 1)

            def gather(tile, parity, earlier):
                if not isinstance(earlier, int) or earlier > 0:
                    pool.wait_ge(s_sw[parity], 16 * earlier)
                nc.gpsimd.tensor_copy(idx[parity][:], ids[:, tile, :]).then_inc(s_idx, 1)
                pool.wait_ge(s_idx, tile + 1)
                pool.sem_inc(s_begun, 1)
                for u in range(4):
                    for n in range(TAB0[u], TAB0[u + 1]):
                        nc.gpsimd.indirect_dma_start(
                            emb[parity][:, n * D:(n + 1) * D], None, tables[n],
                            bass.IndirectOffsetOnAxis(ap=idx[parity][:, n:n + 1], axis=0),
                        ).then_inc(s_gat[parity][u], 16)

            pool.wait_ge(s_ids, 16)
            gather(0, 0, 0)
            gather(1, 1, 0)
            with pool.Fori(1, NTILE // 2) as h:
                gather(2 * h, 0, h)
                gather(2 * h + 1, 1, h)

        @block.tensor
        def _(pe):
            mm, tr = nc.tensor.matmul, nc.tensor.transpose

            pe.wait_ge(s_const, 12)
            pe.wait_ge(s_ld["ws"], 16)
            mm(ps_ab[0][:, 0:D], mean_e[:], ws[:], start=True, stop=True).then_inc(s_p["wsmean"], 1)
            pe.wait_ge(s_ld["wsi"], 16)
            mm(ps_ab[1][0:PROJ, 0:NTAB], mean_p[:], wsi[:], start=True, stop=True).then_inc(s_p["wsimean"], 1)
            pe.wait_ge(s_ld["wd"], 16)
            mm(ps_y[:, 0, 0:D_DENSE], mean_e[:], wd[:], start=True, stop=True).then_inc(s_p["wdmean"], 1)
            pe.wait_ge(s_v["wc"], 1)
            mm(ps_ab[0][:, 0:2 * D], wc2[:], wc2[:], start=True, stop=True).then_inc(s_p["g"], 1)
            pe.wait_ge(s_v["wsi"], 1)
            tr(ps_ab[1][0:GROWS, 0:PROJ], wsc[:].rearrange("p j n -> p (j n)"),
               ident[0:PROJ, 0:PROJ]).then_inc(s_p["wsit"], 1)
            pe.wait_ge(s_v["wd"], 1)
            for k in range(2):
                last = tr(ps_y[:, 1, k * P:(k + 1) * P], wd[:, k * P:(k + 1) * P], ident[:])
            last.then_inc(s_p["wdt"], 1)
            pe.wait_ge(s_v["g"], 1)
            tr(ps_ab[0][:, 0:P], wg2[:], ident[:]).then_inc(s_p["wpt"], 1)
            pe.wait_ge(s_v["wsct"], 1)
            mm(ps_ab[1][:, 0:PROJ], ones[0:NTAB, :], wsct[0:NTAB, :], start=True, stop=True
               ).then_inc(s_p["sc"], 1)
            pe.wait_ge(s_ld["dense"], 16)
            for n in range(2 * NSUPER):
                kc, s = n % 2, n // 2
                if n >= 2:
                    pe.wait_ge(s_a["dense_t"], n - 1)
                bank = (ps_tr, ps_gm)[n % 2]
                for t in range(TPS):
                    last = tr(bank[:, t * P:(t + 1) * P], dense[:, TPS * s + t, kc * P:(kc + 1) * P], ident[:])
                last.then_inc(s_p["dense_t"], 1)
            pe.wait_ge(s_a["dense_t"], 2 * NSUPER)
            pe.wait_ge(s_a["wdt"], 1)
            pe.wait_ge(s_v["wp"], 1)
            pe.wait_ge(s_v["bias"], 1)
            for s in range(NSUPER):
                for kc in range(2):
                    last = mm(x_banks[s], wdt[:, kc, :], dense_t[:, kc, s, :], start=(kc == 0), stop=(kc == 1))
                last.then_inc(s_p["x"], 1)
            for s in range(NSUPER):
                pe.wait_ge(s_a["xsq"], s + 1)
                mm(var_banks[s], mean_e[:], x_sq[:, s, :], start=True, stop=True).then_inc(s_p["xvar"], 1)
            pe.wait_ge(s_ld["wl"], 16)
            pe.wait_ge(s_v["xc"], NSUPER)
            for h in range(2):
                for c in range(4):
                    last = mm(ps_ab[h][:, 0:NPAIR // 2], mean_o[:],
                              wl[:, c, h * (NPAIR // 2):(h + 1) * (NPAIR // 2)], start=(c == 0), stop=(c == 3))
                last.then_inc(s_p["wlmean"], 1)
            pe.wait_ge(s_ld["gsi"], 32)
            pe.wait_ge(s_v["xvar"], NSUPER)
            mm(ps_rf[:, 0:2 * PROJ], ones[0:1, :], gsi_row[:], start=True, stop=True).then_inc(s_p["gb"], 1)

            def sum_of_x():
                pe.wait_ge(s_v["x"], 1)
                for s in range(NSUPER):
                    if s >= 2:
                        pe.wait_ge(s_a["sx"], s - 1)
                    mm(ps_y[0:1, s % 2, :], ones[:, 0:1], xt[:, s, :], start=True, stop=True
                       ).then_inc(s_p["sx"], 1)

            def front_transpose(T, k):
                fk = k + LEAD
                par, u = (fk // UPT) % 2, fk % UPT
                pe.wait_ge(s_gat[par][u], 16 * (TAB0[u + 1] - TAB0[u]) * (2 * T + fk // (2 * UPT) + 1))
                if fk > 0:
                    pe.wait_ge(s_et, UPS * T + fk)
                for m in range(PAIRS[u]):
                    c0 = (TAB0[u] + 2 * m) * D
                    last = tr(ps_tr[:, m * P:(m + 1) * P], emb[par][:, c0:c0 + P], ident[:])
                last.then_inc(s_tr, 1)

            def front_g(T, k):
                fk = k + LEAD
                u = fk % UPT
                pe.wait_ge(s_et, UPS * T + (fk + 1))
                if fk > 0:
                    pe.wait_ge(s_gmr, UPS * T + fk)
                for m in range(PAIRS[u]):
                    last = mm(ps_gm[:, m * P:(m + 1) * P], emb_t[fk % 2][:, m * P:(m + 1) * P], gbd[:],
                              start=True, stop=True)
                last.then_inc(s_gm, 1)

            def gram_product(T, k):
                pe.wait_ge(s_m, UPS * T + (k - 1))
                if k >= 3:
                    pe.wait_ge(s_g2, UPS * T + (k - 2))
                for a_ in range(2):
                    for g in range(4):
                        for j in range(BPG):
                            last = mm(ps_r[PROJ * j:PROJ * (j + 1), 2 * g + a_, :], cen[k % 2][:, a_, g, j, :],
                                      mov[k % 2][:, a_, g, j, :], start=True, stop=True,
                                      tile_position=(0, PROJ * j))
                last.then_inc(s_gr, 1)

            def step(T, k):
                u = k % UPT
                if has_front(T, k):
                    front_transpose(T, k)
                pe.wait_ge(s_xl[u], 16 * (TPS * T + k // UPT + 1))
                if k >= 1:
                    pe.wait_ge(s_qt, UPS * T + k)
                for g in range(4):
                    last = mm(ps_q[:, g * P:(g + 1) * P], xe[u][:, g * P:(g + 1) * P],
                              wbd[:].rearrange("r j p -> r (j p)"), start=True, stop=True)
                last.then_inc(s_q, 1)
                if k >= 2:
                    gram_product(T, k)
                if has_front(T, k):
                    front_g(T, k)
                pe.wait_ge(s_qt, UPS * T + (k + 1))
                for a_ in range(2):
                    if k >= 1:
                        pe.wait_ge(s_c, 2 * UPS * T + (2 * k - 1 + a_))
                    mm(ps_y[:, a_, :], wp[a_][:], qt[k % 2][:], start=True, stop=True).then_inc(s_y, 1)

            def tail(S):
                pe.wait_ge(s_fr, 16 * READS * (S + 1))

                def square_sum(c):
                    pe.wait_ge(s_zc, 4 * S + (c + 1))
                    last = mm(ps_q[:], mean_o[:], z_sq[c % 2], start=(c == 0), stop=(c == 3))
                    if c == 3:
                        last.then_inc(s_ss, 1)

                for c in range(4):
                    if c >= 2:
                        pe.wait_ge(s_zc, 4 * S + (c - 1))
                    for n in range(NFULL):
                        mm(ps_ab[c % 2][:], wl_t[:, n, c * P:(c + 1) * P], f_sb[:, n, :], start=(n == 0), stop=False)
                    mm(ps_ab[c % 2][:], wl_t[0:LASTK, NFULL, c * P:(c + 1) * P], f_last[:, S, :],
                       start=False, stop=True).then_inc(s_z, 1)
                    if c >= 1:
                        square_sum(c - 1)
                for h in range(2):
                    if h == 1:
                        square_sum(3)
                    for kc in range(2):
                        mm(ps_ab[h][:], w1[:, 3 + kc, h * P:(h + 1) * P], dense_t[:, kc, S, :],
                           start=(kc == 0), stop=False)
                pe.wait_ge(s_zs, S + 1)
                for h in range(4):
                    if h >= 2:
                        pe.wait_ge(s_h1r, 4 * S + (h - 1))
                        for kc in range(2):
                            mm(ps_ab[h % 2][:], w1[:, 3 + kc, h * P:(h + 1) * P], dense_t[:, kc, S, :],
                               start=(kc == 0), stop=False)
                    for kc in range(3):
                        last = mm(ps_ab[h % 2][:], w1[:, kc, h * P:(h + 1) * P], z_sb[:, kc, :],
                                  start=False, stop=(kc == 2))
                    last.then_inc(s_h1, 1)
                for h in range(2):
                    for kc in range(4):
                        if h == 0 or kc == 0:
                            pe.wait_ge(s_h1r, 4 * S + max(kc + 1, h + 3))
                        last = mm(ps_ab[h][:], w2[:, kc, h * P:(h + 1) * P], h1_sb[:, kc, :],
                                  start=(kc == 0), stop=(kc == 3))
                    last.then_inc(s_h2, 1)
                for kc in range(2):
                    pe.wait_ge(s_h2r, 2 * S + kc + 1)
                    last = mm(ps_q[0:1, :], w3[:, kc:kc + 1], h2_sb[:, kc, :], start=(kc == 0), stop=(kc == 1))
                last.then_inc(s_yo, 1)
                pe.wait_ge(s_yc, S + 1)

            for k in range(-LEAD, 0):
                front_transpose(0, k)
                front_g(0, k)
            sum_of_x()
            pe.wait_ge(s_a["sx"], NSUPER)
            pe.wait_ge(s_v["gb"], 1)
            pe.wait_ge(s_v["wbd"], 1)
            for c in range(2):
                for k in steps(c):
                    step(0, k)
            pe.wait_ge(s_v["wlrows"], 4)
            for n in range(READS):
                width = P if n < NFULL else LASTK
                if n >= 2:
                    pe.wait_ge(s_a["wlt"], n - 1)
                for c in range(4):
                    last = tr(ps_ab[n % 2][0:width, c * P:(c + 1) * P], wl_x[:, c, n * P:n * P + width], ident[:])
                last.then_inc(s_p["wlt"], 1)
            pe.wait_ge(s_a["wlt"], READS)
            pe.wait_ge(s_ld["w1"], 32)
            pe.wait_ge(s_ld["bl"], 16)
            for h in range(4):
                for kc in range(3):
                    last = mm(ps_ab[0][:, h:h + 1], w1[:, kc, h * P:(h + 1) * P], bl[:, kc:kc + 1],
                              start=(kc == 0), stop=(kc == 2))
            last.then_inc(s_p["b1"], 1)
            pe.wait_ge(s_ld["w2"], 16)
            pe.wait_ge(s_ld["w3"], 16)
            pe.wait_ge(s_v["b1"], 1)
            with pe.Fori(0, NSUPER - 1) as T:
                for c in range(2, 6):
                    for k in steps(c):
                        step(T, k)
                tail(T)
            for c in range(2, 4):
                for k in steps(c):
                    step(NSUPER - 1, k)
            gram_product(NSUPER - 1, UPS)
            gram_product(NSUPER - 1, UPS + 1)
            tail(NSUPER - 1)

        @block.scalar
        def _(act):
            cp = nc.scalar.copy

            act.wait_ge(s_p["wdt"], 1)
            cp(wdt[:].rearrange("p k e -> p (k e)"), ps_y[:, 1, 0:2 * P]).then_inc(s_a["wdt"], 1)
            for n in range(2 * NSUPER):
                kc, s = n % 2, n // 2
                act.wait_ge(s_p["dense_t"], n + 1)
                cp(dense_t[:, kc, s, :].rearrange("k (j g) -> k g j", j=BPG),
                   (ps_tr, ps_gm)[n % 2][:].rearrange("k (g j) -> k g j", j=BPG)).then_inc(s_a["dense_t"], 1)
            for s in range(NSUPER):
                act.wait_ge(s_v["xc"], s + 1)
                nc.scalar.activation(x_sq[:, s, :], xt[:, s, :], ACT.Square).then_inc(s_a["xsq"], 1)
            act.wait_ge(s_v["xrr"], 1)
            nc.scalar.activation(x_rs, x_rr, ACT.Sqrt).then_inc(s_a["xrs"], 1)

            def sum_of_x():
                for s in range(NSUPER):
                    act.wait_ge(s_p["sx"], s + 1)
                    cp(f_last[2 * PROJ:LASTK, s, :], ps_y[0:1, s % 2, :]).then_inc(s_a["sx"], 1)

            def front_copy(T, k):
                fk = k + LEAD
                w = PAIRS[fk % UPT] * P
                act.wait_ge(s_tr, UPS * T + (fk + 1))
                if fk >= 2:
                    act.wait_ge(s_gm, UPS * T + (fk - 1))
                cp(emb_t[fk % 2][:, 0:w], ps_tr[:, 0:w]).then_inc(s_et, 1)

            def front_sqrt(T, k):
                fk = k + LEAD
                if fk % UPT == UPT - 1:
                    act.wait_ge(s_vbr, TPS * T + fk // UPT + 1)
                    nc.scalar.activation(rs_b[:], var_r[:], ACT.Sqrt).then_inc(s_rb, 1)

            def gram_copy(T, k):
                act.wait_ge(s_gr, UPS * T + (k - 1))
                if (k - 2) % UPS == 0 and k > 2:
                    act.wait_ge(s_fw, 16 * WRITES * (T + (k - 2) // UPS))
                g0 = (T * GPS + (k - 2) * GPU) % (2 * GPS)
                cp(gram[:, :, bass.ds(g0, GPU)], ps_r.rearrange("p g q -> p q g")).then_inc(s_g2, 1)

            def step(T, k):
                if has_front(T, k):
                    front_copy(T, k)
                act.wait_ge(s_q, UPS * T + (k + 1))
                if k >= 2:
                    act.wait_ge(s_y, 2 * UPS * T + (2 * k - 2))
                cp(qt[k % 2][:], ps_q[:]).then_inc(s_qt, 1)
                if k >= 2:
                    gram_copy(T, k)
                act.wait_ge(s_c, 2 * UPS * T + (2 * k + 2))
                if k >= 1:
                    act.wait_ge(s_v2, UPS * T + k)
                nc.scalar.activation(sq[:], cen[k % 2][:], ACT.Square).then_inc(s_sq, 1)
                act.wait_ge(s_r2, UPS * T + (k + 1))
                nc.scalar.activation(mov[k % 2][:, :, :, :, QN - 1], r2[:], ACT.Sqrt).then_inc(s_rs, 1)
                if has_front(T, k):
                    front_sqrt(T, k)

            def tail(S):
                for c in range(4):
                    act.wait_ge(s_z, 4 * S + (c + 1))
                    if c < 3:
                        nc.scalar.activation(z_c[:, c, :], ps_ab[c % 2][:], ACT.Identity,
                                             bias=const_z[:, c:c + 1])
                    nc.scalar.activation(z_sq[c % 2], ps_ab[c % 2][:], ACT.Square,
                                         bias=const_z[:, c:c + 1]).then_inc(s_zc, 1)
                act.wait_ge(s_zr, S + 1)
                nc.scalar.activation(rz_sb, rz_v, ACT.Sqrt).then_inc(s_rz, 1)
                for h in range(4):
                    act.wait_ge(s_h1, 4 * S + h + 1)
                    nc.scalar.activation(h1_sb[:, h, :], ps_ab[h % 2][:], ACT.Relu,
                                         bias=b1x[:, h:h + 1]).then_inc(s_h1r, 1)
                for h in range(2):
                    act.wait_ge(s_h2, 2 * S + h + 1)
                    nc.scalar.activation(h2_sb[:, h, :], ps_ab[h][:], ACT.Relu,
                                         bias=b2[:, h:h + 1]).then_inc(s_h2r, 1)
                act.wait_ge(s_yo, S + 1)
                act.wait_ge(s_out, 16 * (S + 1))
                cp(y_sb.rearrange("o (g j) -> o g j", j=BPG),
                   ps_q[0:1, :].rearrange("o (j g) -> o g j", j=BPG)).then_inc(s_yc, 1)
                act.wait_ge(s_yc, S + 1)
                act.dma_start(out[bass.ds(S * SUPER, SUPER), :].rearrange("(o b) c -> o (b c)", o=1), y_sb
                              ).then_inc(s_out, 16)

            for k in range(-LEAD, 0):
                front_copy(0, k)
                front_sqrt(0, k)
            sum_of_x()
            for c in range(2):
                for k in steps(c):
                    step(0, k)
            for n in range(READS):
                width = P if n < NFULL else LASTK
                act.wait_ge(s_p["wlt"], n + 1)
                cp(wl_t[0:width, n, :], ps_ab[n % 2][0:width, :]).then_inc(s_a["wlt"], 1)
            act.wait_ge(s_ld["b2"], 16)
            act.wait_ge(s_v["b1"], 1)
            act.sem_inc(s_out, 16)
            with act.Fori(0, NSUPER - 1) as T:
                for c in range(2, 6):
                    for k in steps(c):
                        step(T, k)
                tail(T)
            for c in range(2, 4):
                for k in steps(c):
                    step(NSUPER - 1, k)
            gram_copy(NSUPER - 1, UPS)
            gram_copy(NSUPER - 1, UPS + 1)
            tail(NSUPER - 1)
            act.wait_ge(s_out, 16 * (NSUPER + 1))

        @block.vector
        def _(dve):
            tt, ts = nc.vector.tensor_tensor, nc.vector.tensor_scalar
            chain = [0]

            def link(ins):
                chain[0] += 1
                ins.then_inc(s_chain, 1)
                dve.wait_ge(s_chain, chain[0])

            dve.wait_ge(s_p["wsmean"], 1)
            for h in range(2):
                last = tt(wc2[:, h * D:(h + 1) * D], ws[:], ps_ab[0][:, 0:D], ALU.subtract)
            last.then_inc(s_v["wc"], 1)
            dve.wait_ge(s_p["wsimean"], 1)
            for j in range(BPG):
                last = tt(wsc[:, j, :], wsi[:], ps_ab[1][0:PROJ, 0:NTAB], ALU.subtract)
            last.then_inc(s_v["wsi"], 1)
            dve.wait_ge(s_p["wdmean"], 1)
            tt(wd[:], wd[:], ps_y[:, 0, 0:D_DENSE], ALU.subtract).then_inc(s_v["wd"], 1)
            dve.wait_ge(s_p["g"], 1)
            dve.wait_ge(s_const, 12)
            dve.wait_ge(s_ld["vec"], 64)
            dve.wait_ge(s_v["wc"], 1)
            for h in range(2):
                r = slice(h * D, (h + 1) * D)
                ts(gbd[r, r], ps_ab[0][r, r], 1.0 / E_DIM, None, ALU.mult)
            ts(wg2[:], wc2[:], vec[:, 0:1], None, ALU.mult).then_inc(s_v["g"], 1)
            dve.wait_ge(s_p["wsit"], 1)
            nc.vector.tensor_copy(wsct[:], ps_ab[1][0:GROWS, 0:PROJ]).then_inc(s_v["wsct"], 1)
            dve.wait_ge(s_v["wsct"], 1)
            for j in range(BPG):
                last = ts(wbd[:, j, :], wsct[:], group_mask[:, j:j + 1], None, ALU.mult)
            last.then_inc(s_v["wbd"], 1)
            dve.wait_ge(s_p["wpt"], 1)
            nc.vector.tensor_copy(wp[0][0:D, :], ps_ab[0][0:D, 0:P])
            nc.vector.tensor_copy(wp[1][D:2 * D, :], ps_ab[0][D:2 * D, 0:P]).then_inc(s_v["wp"], 1)
            dve.wait_ge(s_p["sc"], 1)
            ts(bias_y[:], ps_ab[1][:, 0:PROJ], vec[:, 1:2], None, ALU.mult).then_inc(s_v["bias"], 1)
            for s in range(NSUPER):
                dve.wait_ge(s_p["x"], s + 1)
                nc.vector.tensor_copy(xt[:, s, :], x_banks[s]).then_inc(s_v["xc"], 1)
            for s in range(NSUPER):
                dve.wait_ge(s_p["xvar"], s + 1)
                ts(x_rs[:, s, :], var_banks[s], EPS, None, ALU.add).then_inc(s_v["xvar"], 1)
            dve.wait_ge(s_v["xvar"], NSUPER)
            nc.vector.reciprocal(x_rr, x_rs).then_inc(s_v["xrr"], 1)
            for h in range(2):
                dve.wait_ge(s_p["wlmean"], h + 1)
                for c in range(4):
                    r = slice(h * (NPAIR // 2), (h + 1) * (NPAIR // 2))
                    last = tt(wl[:, c, r], wl[:, c, r], ps_ab[h][:, 0:NPAIR // 2], ALU.subtract)
            last.then_inc(s_v["wlsub"], 1)
            dve.wait_ge(s_p["gb"], 1)
            nc.vector.tensor_copy(gb[:], ps_rf[:, 0:2 * PROJ]).then_inc(s_v["gb"], 1)
            dve.wait_ge(s_a["xrs"], 1)
            link(nc.vector.scalar_tensor_tensor(out=xt[:], in0=xt[:], scalar=vec[:, 2:3], in1=x_rs,
                                                op0=ALU.mult, op1=ALU.mult))
            ts(xt[:], xt[:], vec[:, 3:4], None, ALU.add).then_inc(s_v["x"], 1)

            def low_rows():
                link(nc.vector.memset(wl_low[:], 0.0))
                dve.wait_ge(s_v["wlsub"], 1)
                for p in range(PROJ):
                    r0 = p * (p + 1) // 2
                    last = nc.vector.tensor_copy(wl_low[:, :, 0:p + 1, p], wl[:, :, r0:r0 + p + 1])
                link(last)
                dve.wait_ge(s_v["gb"], 1)

            def weight_rows(c):
                low_c = wl_low[:, c]
                gsi, bsi = gb[:, 0:PROJ], gb[:, PROJ:]
                over_q = [P, PROJ + 1, PROJ]
                link(tt(prep_tmp[:], low_c, bsi.unsqueeze(1).to_broadcast(over_q), ALU.mult))
                link(nc.vector.tensor_reduce(small[:, 0, :], prep_tmp[:], AX.X, ALU.add))
                link(tt(prep_tmp[:, 0:PROJ, :], low_c[:, 1:, :],
                        bsi.unsqueeze(2).to_broadcast([P, PROJ, PROJ]), ALU.mult))
                link(nc.vector.tensor_reduce(small[:, 1, 0:PROJ],
                                             prep_tmp[:, 0:PROJ, :].rearrange("o q p -> o p q"), AX.X, ALU.add))
                link(tt(small[:, 2, 0:PROJ], small[:, 0, 1:], bsi, ALU.mult))
                link(nc.vector.tensor_reduce(const_z[:, c:c + 1], small[:, 2, 0:PROJ], AX.X, ALU.add))
                link(ts(const_z[:, c:c + 1], const_z[:, c:c + 1], float(E_DIM), None, ALU.mult))
                link(tt(small[:, 3, 0:PROJ], small[:, 0, 1:], small[:, 1, 0:PROJ], ALU.add))
                r = NFULL * P
                tt(wl_x[:, c, r + PROJ:r + 2 * PROJ], small[:, 3, 0:PROJ], gsi, ALU.mult)
                nc.vector.tensor_copy(wl_x[:, c, r + 2 * PROJ:r + LASTK], small[:, 0, 0:1])
                link(tt(low_c, low_c, gsi.unsqueeze(1).to_broadcast(over_q), ALU.mult))
                nc.vector.tensor_copy(wl_x[:, c, r:r + PROJ], low_c[:, 0, :])
                for row, q0, nq, p0, np_ in BLOCKS:
                    last = tt(wl_x[:, c, row:row + nq * np_].rearrange("o (q p) -> o q p", q=nq),
                              low_c[:, 1 + q0:1 + q0 + nq, p0:p0 + np_],
                              gsi[:, q0:q0 + nq].unsqueeze(2).to_broadcast([P, nq, np_]), ALU.mult)
                last.then_inc(s_v["wlrows"], 1)

            def front_var(T, k):
                fk = k + LEAD
                par, u = (fk // UPT) % 2, fk % UPT
                w = PAIRS[u] * P
                dve.wait_ge(s_gm, UPS * T + (fk + 1))
                tt(prod[fk % 2][:, 0:w], ps_gm[:, 0:w], emb[par][:, TAB0[u] * D:TAB0[u] * D + w], ALU.mult
                   ).then_inc(s_gmr, 1)
                dve.wait_ge(s_gmr, UPS * T + (fk + 1))
                nc.vector.tensor_reduce(var_b[:, TAB0[u]:TAB0[u + 1]],
                                        prod[fk % 2][:, 0:w].rearrange("b (n d) -> b n d", d=D), AX.X, ALU.add
                                        ).then_inc(s_vb, 1)

            def front_scale(T, k):
                fk = k + LEAD
                par = (fk // UPT) % 2
                if fk % UPT == UPT - 1:
                    tile = TPS * T + fk // UPT
                    dve.wait_ge(s_vb, UPS * T + (fk + 1))
                    ts(var_e[:], var_b[:], EPS, None, ALU.add).then_inc(s_vbe, 1)
                    dve.wait_ge(s_vbe, tile + 1)
                    nc.vector.reciprocal(var_r[:], var_e[:]).then_inc(s_vbr, 1)
                    dve.wait_ge(s_rb, tile + 1)
                    e = emb[par][:].rearrange("b (n d) -> b n d", d=D)
                    tt(e, e, rs_b[:].unsqueeze(2).to_broadcast([P, NTAB, D]), ALU.mult).then_inc(s_sc, 1)

            def step(T, k):
                i = UPS * T + k
                p = k % 2
                for a_ in range(2):
                    dve.wait_ge(s_y, 2 * UPS * T + (2 * k + a_ + 1))
                    if a_ == 0 and k >= 2:
                        dve.wait_ge(s_gr, UPS * T + (k - 1))
                    tt(cen[p][:, a_].rearrange("e g j p -> e (g j) p"),
                       ps_y[:, a_, :].rearrange("e (b p) -> e b p", p=PROJ),
                       bias_y[:].unsqueeze(1).to_broadcast([P, UNIT // 2, PROJ]), ALU.add).then_inc(s_c, 1)
                if has_front(T, k):
                    front_var(T, k)
                dve.wait_ge(s_sq, i + 1)
                nc.vector.tensor_reduce(v2[:], sq[:].rearrange("e a g j p -> e (a g j) p"), AX.X, ALU.add
                                        ).then_inc(s_v2, 1)
                dve.wait_ge(s_v2, i + 1)
                ts(v2e[:], v2[:], 1.0 / PROJ, EPS, ALU.mult, ALU.add).then_inc(s_v2e, 1)
                dve.wait_ge(s_v2e, i + 1)
                nc.vector.reciprocal(r2[:].rearrange("e a g j -> e (a g j)"), v2e[:]).then_inc(s_r2, 1)
                dve.wait_ge(s_r2, i + 1)
                m = mov[p][:].rearrange("e a g j q -> e (a g j) q")
                tt(m[:, :, 0:PROJ], cen[p][:].rearrange("e a g j p -> e (a g j) p"),
                   r2[:].rearrange("e a g j -> e (a g j)").unsqueeze(2).to_broadcast([P, UNIT, PROJ]), ALU.mult)
                dve.wait_ge(s_rs, i + 1)
                S, g0 = T + k // UPS, (k % UPS) * GPU
                x = xt[:, S, :].rearrange("e (j g) -> e j g", j=BPG)[:, :, g0:g0 + GPU]
                x = x.rearrange("e j (g a) -> e a g j", a=2)
                for a_ in range(2):
                    last = tt(mov[p][:, a_, :, :, PROJ], mov[p][:, a_, :, :, PROJ + 1], x[:, a_], ALU.mult)
                last.then_inc(s_m, 1)
                if has_front(T, k):
                    front_scale(T, k)

            def tail(S):
                dve.wait_ge(s_ss, S + 1)
                ts(rz_sb, ps_q[:], EPS, None, ALU.add).then_inc(s_zv, 1)
                dve.wait_ge(s_zv, S + 2)
                nc.vector.reciprocal(rz_v, rz_sb).then_inc(s_zr, 1)
                dve.wait_ge(s_rz, S + 1)
                for c in range(3):
                    last = nc.vector.scalar_tensor_tensor(out=z_sb[:, c, :], in0=z_c[:, c, :], scalar=gl[:, c:c + 1],
                                                          in1=rz_sb, op0=ALU.mult, op1=ALU.mult)
                last.then_inc(s_zs, 1)

            for k in range(-LEAD, 0):
                front_var(0, k)
                front_scale(0, k)
            for c in range(2):
                for k in steps(c):
                    step(0, k)
                    if k == 0:
                        low_rows()
                    elif k <= 4:
                        weight_rows(k - 1)
            dve.wait_ge(s_p["b1"], 1)
            dve.wait_ge(s_ld["b1"], 16)
            tt(b1x[:], ps_ab[0][:, 0:4], b1[:], ALU.add).then_inc(s_v["b1"], 1)
            dve.wait_ge(s_ld["gl"], 16)
            dve.sem_inc(s_zv, 1)
            with dve.Fori(0, NSUPER - 1) as T:
                for c in range(2, 6):
                    for k in steps(c):
                        step(T, k)
                tail(T)
            for c in range(2, 4):
                for k in steps(c):
                    step(NSUPER - 1, k)
            tail(NSUPER - 1)


_NAMES = (["r_dense_t", "ids"] + [f"tbl_{n}" for n in range(NTAB)]
          + ["W_top1", "b_top1", "W_top2", "b_top2", "W_top3"]
          + [f"L0_rec_{n}" for n in ("Wd", "gd", "bd", "Ws", "gs", "bs", "Wsi", "gsi", "bsi", "Wl", "gl", "bl")])


def kernel(**inputs):
    import numpy as np
    import concourse.bacc as bacc
    from concourse.bass_utils import run_bass_kernel_spmd

    nc = bacc.Bacc("TRN2", target_bir_lowering=False, num_devices=1)
    arrays, args = {}, {}
    for name in _NAMES:
        x = np.ascontiguousarray(inputs[name])
        arrays[f"in_{name}"] = x
        args[name] = nc.dram_tensor(f"in_{name}", x.shape, mybir.dt.from_np(x.dtype), kind="ExternalInput").ap()
    out = nc.dram_tensor("out_y", (ROWS, 1), F32, kind="ExternalOutput").ap()
    interaction_tower(nc, args, out)
    r = run_bass_kernel_spmd(nc, [arrays], core_ids=[0])
    return r.results[0]["out_y"]
```

```python
from contextlib import ExitStack

import concourse.bass as bass
from concourse import mybir

F32 = mybir.dt.float32
BF16 = mybir.dt.bfloat16
I32 = mybir.dt.int32
ALU = mybir.AluOpType
ACT = mybir.ActivationFunctionType
AX = mybir.AxisListType

ROWS = 2048
NTAB, D = 26, 64
E_DIM, PROJ = 128, 32
D_DENSE = 256
MAXD, USED = 512, 384
H1, H2 = 512, 256
NPAIR = (PROJ + 1) * PROJ // 2
EPS = 1e-5
P = 128

TILE = 128
NTILE = ROWS // TILE
UNIT = 32
UPT = TILE // UNIT
SUPER = 512
TPS = SUPER // TILE
NSUPER = ROWS // SUPER
BPG = 4
GROWS = BPG * NTAB
GPU = UNIT // BPG
GPS = SUPER // BPG
UPS = TPS * UPT
UPP = 2 * UPT
NUNIT = ROWS // UNIT
LEAD = 6

PAIRS = [4, 3, 3, 3]
TAB0 = [0, 8, 14, 20, 26]
QN = PROJ + 2

BLOCKS = [(0, 0, 16, 16, 16)]
BLOCKS += [(256 + 64 * h, 16 * h, 8, 16 * h + 8, 8) for h in range(2)]
BLOCKS += [(384 + 64 * t, 8 * t, 8, 8 * t, 8) for t in range(4)]
NFULL = 5
LASTK = 2 * PROJ + 1
WRITES = BPG * (len(BLOCKS) + 1)
READS = NFULL + 1


def interaction_tower(nc, a, out):
    tables = [a[f"tbl_{n}"] for n in range(NTAB)]
    scaled_d = nc.dram_tensor("scaled_d", (NTILE, TILE * NTAB, D), F32, kind="Internal").ap()
    gram_d = nc.dram_tensor("gram_d", (NSUPER, NFULL * P + 2 * PROJ, BPG, GPS), F32, kind="Internal").ap()

    with ExitStack() as ctx:
        ctx.enter_context(nc.allow_non_contiguous_dma(reason="bias vectors, once"))

        def sb(name, shape, dt=F32):
            return ctx.enter_context(nc.sbuf_tensor(name, shape, dt))

        def pb(name, shape):
            return ctx.enter_context(nc.psum_tensor(name, shape, F32))

        def sem(name):
            return ctx.enter_context(nc.semaphore(name))

        ps_tr = pb("ps_tr", [P, 512])
        ps_gm = pb("ps_gm", [P, 512])
        ps_q = pb("ps_q", [P, 512])
        ps_y = pb("ps_y", [P, 2, 512])
        ps_rf = pb("ps_r", [P, 512])
        ps_r = ps_rf[:, 0:GPU * QN].rearrange("p (g q) -> p g q", q=QN)
        ps_ab = [pb("ps_a", [P, 512]), pb("ps_b", [P, 512])]

        ident = sb("ident", [P, P])
        ones = sb("ones", [P, P])
        mean_e = sb("mean_e", [P, P])
        mean_o = sb("mean_o", [P, P])
        mean_p = sb("mean_p", [PROJ, PROJ])
        group_mask = sb("group_mask", [GROWS, BPG])

        ws = sb("ws", [P, D])
        wsi = sb("wsi", [PROJ, NTAB])
        vec = sb("vec", [P, 4])
        gsi_row = sb("gsi_row", [1, 2 * PROJ])
        w1 = sb("w1", [P, 5, H1])
        w2 = sb("w2", [P, 4, H2])
        w3 = sb("w3", [P, 2])
        b1 = sb("b1", [P, 4])
        b2 = sb("b2", [P, 2])
        gl = sb("gl", [P, 3])
        bl = sb("bl", [P, 3])
        wl = sb("wl", [P, 4, NPAIR])

        gbd = sb("gbd", [P, P])
        wp = [sb("wp0", [P, E_DIM]), sb("wp1", [P, E_DIM])]
        wsc = sb("wsc", [PROJ, BPG, NTAB])
        wsct = sb("wsct", [GROWS, PROJ])
        wbd = sb("wbd", [GROWS, BPG, PROJ])
        bias_y = sb("bias_y", [P, PROJ])
        bias_h = sb("bias_h", [PROJ, E_DIM], BF16)
        bias_t = sb("bias_t", [3 * PROJ, E_DIM], BF16)
        select = sb("select", [3 * PROJ, 512 // PROJ, PROJ], BF16)
        wdt = sb("wdt", [P, 2, E_DIM])
        gb = sb("gb", [P, 2 * PROJ])
        wl_low = sb("wl_low", [P, 4, PROJ + 1, PROJ])
        wl_x = sb("wl_x", [P, 4, NFULL * P + LASTK])
        wl_t = sb("wl_t", [P, READS, MAXD])
        const_z = sb("const_z", [P, 4])
        b1x = sb("b1x", [P, 4])
        small = sb("small", [P, 4, PROJ + 1])

        ids = sb("ids", [P, NTILE, NTAB], I32)
        idx = [sb(f"idx{i}", [P, NTAB], I32) for i in range(2)]
        emb = [sb(f"emb{i}", [P, NTAB * D]) for i in range(2)]
        emb_t = [sb(f"emb_t{i}", [P, 512]) for i in range(2)]
        prod = [sb(f"prod{i}", [P, 512]) for i in range(2)]
        var_b = sb("var_b", [P, NTAB])
        var_e = sb("var_e", [P, NTAB])
        var_r = sb("var_r", [P, NTAB])
        rs_b = sb("rs_b", [P, NTAB])
        xe = [sb(f"xe{u}", [GROWS, GPU * D]) for u in range(UPT)]
        qt = [sb(f"qt{i}", [P, 512]) for i in range(2)]
        cen = [sb(f"cen{i}", [P, 2, 4, BPG, PROJ]) for i in range(2)]
        sq = sb("sq", [P, 2, 4, BPG, PROJ])
        mov = [sb(f"mov{i}", [P, 2, 4, BPG, QN]) for i in range(2)]
        v2 = sb("v2", [P, UNIT])
        v2e = sb("v2e", [P, UNIT])
        r2 = sb("r2", [P, 2, 4, BPG])
        gram = sb("gram", [P, QN, 2 * GPS])
        f_sb = sb("f_sb", [P, NFULL, SUPER])
        f_last = sb("f_last", [LASTK, NSUPER, SUPER])
        dense_t = sb("dense_t", [P, 2, BPG, ROWS // BPG])
        xt = sb("xt", [P, BPG, ROWS // BPG])
        prep_tmp = sb("prep_tmp", [P, PROJ + 1, PROJ])

        ring = gram[:].rearrange("p q g -> p (q g)")
        dense = ring[:, 0:NTILE * D_DENSE].rearrange("p (t k) -> p t k", t=NTILE)
        x_sq = ring[:, 2 * ROWS:3 * ROWS].rearrange("p (j g) -> p j g", j=BPG)
        x_rs = ring[:, 3 * ROWS:4 * ROWS].rearrange("p (j g) -> p j g", j=BPG)
        x_rr = x_sq
        spare = ring[:, 4 * ROWS:]
        wd = spare[:, 0:D_DENSE]
        wc2 = spare[:, D_DENSE:D_DENSE + 2 * D]
        wg2 = spare[:, D_DENSE + 2 * D:D_DENSE + 4 * D]
        bias_r = mov[0][:].rearrange("p a g j q -> p (a g j q)")[0:PROJ, 0:2 * E_DIM].rearrange(
            "p (n e) -> p n e", n=2)
        low = wl_low[:].rearrange("p c q k -> p (c q k)")
        z_c = low[:, 0:1536].rearrange("p (c b) -> p c b", c=3)
        z_sq = low[:, 1536:3584].rearrange("p (c b) -> p c b", c=4)
        rz_sb = low[:, 3584:4096]
        old_wl = wl[:].rearrange("p c k -> p (c k)")
        z_sb = old_wl[:, 0:1536].rearrange("p (c b) -> p c b", c=3)
        rz_v = old_wl[:, 1536:2048]
        old_wl_x = wl_x[:].rearrange("p c k -> p (c k)")
        h1_sb = old_wl_x[:, 0:4 * SUPER].rearrange("p (c b) -> p c b", c=4)
        y_sb = old_wl_x[0:1, 4 * SUPER:5 * SUPER]
        h2_sb = prep_tmp[:].rearrange("p q k -> p (q k)")[:, 0:2 * SUPER].rearrange("p (c b) -> p c b", c=2)

        s_const = sem("const_ready")
        s_ld = {n: sem(f"ld_{n}") for n in ("ws", "wd", "wsi", "vec", "gsi", "w1", "w2", "w3", "b1", "b2",
                                            "gl", "bl", "wl", "dense")}
        s_ids = sem("ids_loaded")
        s_idx = sem("tile_ids_ready")
        s_begun = sem("gather_tiles_begun")
        s_gat = [[sem(f"gathered{i}_{u}") for u in range(4)] for i in range(2)]
        s_sw = [sem(f"scaled_written{i}") for i in range(2)]
        s_xl = [sem(f"unit_loaded{u}") for u in range(UPT)]
        s_fw = sem("gram_written")
        s_fr = sem("gram_read_back")
        s_out = sem("out_written")
        s_p = {n: sem(f"prep_p_{n}") for n in ("wsmean", "wsimean", "wdmean", "g", "wsit", "wdt", "wpt", "sc", "biast",
                                               "dense_t", "x", "xvar", "wlmean", "gb", "sx", "wlt", "b1")}
        s_a = {n: sem(f"prep_a_{n}") for n in ("wdt", "dense_t", "xsq", "xrs", "sx", "wlt")}
        s_v = {n: sem(f"prep_v_{n}") for n in ("wc", "wsi", "wd", "g", "wsct", "wbd", "wp", "bias", "bias3", "xc", "xvar",
                                               "xrr", "x", "wlsub", "gb", "wlrows", "b1")}
        s_tr = sem("emb_transposed")
        s_gm = sem("emb_g_ready")
        s_q = sem("q_ready")
        s_y = sem("y_ready")
        s_gr = sem("gram_ready")
        s_z = sem("z_ready")
        s_ss = sem("z_square_sum_ready")
        s_h1 = sem("h1_ready")
        s_h2 = sem("h2_ready")
        s_yo = sem("y_out_ready")
        s_et = sem("emb_t_copied")
        s_qt = sem("qt_copied")
        s_sq = sem("squared")
        s_rs = sem("r_ready")
        s_g2 = sem("gram_copied")
        s_rb = sem("emb_r_ready")
        s_zc = sem("z_copied")
        s_rz = sem("z_r_ready")
        s_h1r = sem("h1_relu")
        s_h2r = sem("h2_relu")
        s_yc = sem("y_copied")
        s_chain = sem("prep_chain")
        s_gmr = sem("emb_product_ready")
        s_vb = sem("emb_var_part")
        s_vbe = sem("emb_var_eps")
        s_vbr = sem("emb_var_reciprocal")
        s_sc = sem("emb_scaled")
        s_c = sem("centred_ready")
        s_v2 = sem("feature_var")
        s_v2e = sem("feature_var_eps")
        s_r2 = sem("feature_r2")
        s_m = sem("moving_ready")
        s_zv = sem("z_var_eps")
        s_zr = sem("z_var_reciprocal")
        s_zs = sem("z_scaled")

        def unit(H, k):
            return not isinstance(H, int) or 0 <= UPP * H + k < NUNIT

        def super_of(x, S):
            return x[:, :, bass.ds(S * GPS, GPS)]

        x_banks = [ps_y[:, 0, :], ps_y[:, 1, :], ps_ab[0][:], ps_ab[1][:]]
        var_banks = [ps_tr[:], ps_gm[:], ps_q[:], ps_rf[:]]

        block = ctx.enter_context(nc.Block())

        @block.sync
        def _(sp):
            def load(dst, src, name):
                sp.dma_start(dst, src).then_inc(s_ld[name], 16)

            def write_scaled(tile, parity):
                sp.wait_ge(s_sc, tile + 1)
                sp.dma_start(scaled_d[tile].rearrange("(b n) d -> b (n d)", n=NTAB),
                             emb[parity][:]).then_inc(s_sw[parity], 16)

            def load_unit(tile, parity, nth, u, first=False):
                if u == 0:
                    sp.wait_ge(s_sw[parity], 16 * nth)
                if not first:
                    sp.wait_ge(s_q, tile * UPT + (u - UPT + 1))
                src = scaled_d[tile][u * GPU * GROWS:(u + 1) * GPU * GROWS, :].rearrange(
                    "(g r) d -> r g d", r=GROWS)
                sp.dma_start(xe[u][:].rearrange("r (g d) -> r g d", g=GPU), src).then_inc(s_xl[u], 16)

            def write_gram(S):
                sp.wait_ge(s_g2, UPS * S + UPS)
                g0 = (S * GPS) % (2 * GPS)
                for j in range(BPG):
                    for row, q0, nq, p0, np_ in BLOCKS:
                        sp.dma_start(
                            gram_d[S][row:row + nq * np_, j, :].rearrange("(q p) g -> p q g", q=nq),
                            gram[PROJ * j + p0:PROJ * j + p0 + np_, q0:q0 + nq, bass.ds(g0, GPS)],
                        ).then_inc(s_fw, 16)
                    sp.dma_start(
                        gram_d[S][NFULL * P:, j, :].rearrange("(q p) g -> p q g", q=2),
                        gram[PROJ * j:PROJ * (j + 1), PROJ:QN, bass.ds(g0, GPS)],
                    ).then_inc(s_fw, 16)

            def read_gram(S):
                if not isinstance(S, int) or S > 0:
                    sp.wait_ge(s_z, 4 * S)
                sp.wait_ge(s_fw, 16 * WRITES * (S + 1))
                for c in range(NFULL):
                    sp.dma_start(f_sb[:, c, :], gram_d[S][c * P:(c + 1) * P].rearrange("r j g -> r (j g)")
                                 ).then_inc(s_fr, 16)
                sp.dma_start(f_last[0:2 * PROJ, S, :], gram_d[S][NFULL * P:].rearrange("r j g -> r (j g)")
                             ).then_inc(s_fr, 16)

            def feed(H, c, S=None):
                tile, parity, nth = 2 * H + c, c % 2, H + (c // 2 + 1)
                write_scaled(tile, parity)
                for u in range(UPT - 1):
                    load_unit(tile, parity, nth, u)
                if S is not None:
                    write_gram(S)
                load_unit(tile, parity, nth, UPT - 1)
                if S is not None:
                    read_gram(S)

            sp.dma_start(ids[:], a["ids"].rearrange("(t p) n -> p t n", p=TILE)).then_inc(s_ids, 16)
            load(ws[:], a["L0_rec_Ws"], "ws")
            for n, v in enumerate(("gs", "bs", "gd", "bd")):
                load(vec[:, n:n + 1], a[f"L0_rec_{v}"].rearrange("(e o) -> e o", o=1), "vec")
            load(wsi[:], a["L0_rec_Wsi"], "wsi")
            load(wd, a["L0_rec_Wd"], "wd")
            load(dense, a["r_dense_t"].rearrange("(t p) k -> p t k", p=TILE), "dense")
            load(gsi_row[:, 0:PROJ], a["L0_rec_gsi"].rearrange("(o p) -> o p", o=1), "gsi")
            load(gsi_row[:, PROJ:], a["L0_rec_bsi"].rearrange("(o p) -> o p", o=1), "gsi")
            load(wl[:], a["L0_rec_Wl"].rearrange("(c o) k -> o c k", o=P), "wl")
            load(w1[:, 0:3, :], a["W_top1"][0:USED, :].rearrange("(c k) h -> k c h", k=P), "w1")
            load(w1[:, 3:5, :], a["W_top1"][MAXD:, :].rearrange("(c k) h -> k c h", k=P), "w1")
            load(bl[:], a["L0_rec_bl"][0:USED].rearrange("(c o) -> o c", o=P), "bl")
            load(gl[:], a["L0_rec_gl"][0:USED].rearrange("(c o) -> o c", o=P), "gl")
            load(b1[:], a["b_top1"].rearrange("(c o) -> o c", o=P), "b1")
            load(w2[:], a["W_top2"].rearrange("(c k) h -> k c h", k=P), "w2")
            load(b2[:], a["b_top2"].rearrange("(c o) -> o c", o=P), "b2")
            load(w3[:], a["W_top3"].rearrange("(c k) o -> k (c o)", k=P), "w3")

            write_scaled(0, 0)
            for u in range(UPT):
                load_unit(0, 0, 1, u, first=True)
            feed(0, 1)
            with sp.Fori(0, 2) as H:
                feed(H, 2)
                feed(H, 3)
            write_gram(0)
            read_gram(0)
            with sp.Fori(0, 2) as T:
                feed(2 * T + 2, 2)
                feed(2 * T + 2, 3)
                feed(2 * T + 2, 4)
                feed(2 * T + 2, 5, S=T + 1)
            feed(6, 2)
            feed(6, 3)
            write_gram(NSUPER - 1)
            read_gram(NSUPER - 1)

        @block.gpsimd
        def _(pool):
            nc.gpsimd.memset(ident[:], 0.0).then_inc(s_const, 1)
            nc.gpsimd.memset(group_mask[:], 1.0).then_inc(s_const, 1)
            nc.gpsimd.memset(ones[:], 1.0).then_inc(s_const, 1)
            nc.gpsimd.memset(mean_e[:], 1.0 / E_DIM).then_inc(s_const, 1)
            nc.gpsimd.memset(mean_o[:], 1.0 / MAXD).then_inc(s_const, 1)
            nc.gpsimd.memset(mean_p[:], 1.0 / PROJ).then_inc(s_const, 1)
            nc.gpsimd.memset(gbd[:], 0.0).then_inc(s_const, 1)
            nc.gpsimd.memset(wp[0][:], 0.0).then_inc(s_const, 1)
            nc.gpsimd.memset(wp[1][:], 0.0).then_inc(s_const, 1)
            pool.wait_ge(s_const, 9)
            nc.gpsimd.affine_select(out=ident[:], in_=ident[:], compare_op=ALU.not_equal, fill=1.0, base=0,
                                    pattern=[[-1, P]], channel_multiplier=1).then_inc(s_const, 1)
            nc.gpsimd.affine_select(out=group_mask[:], in_=group_mask[:], compare_op=ALU.is_ge, fill=0.0, base=0,
                                    pattern=[[-NTAB, BPG]], channel_multiplier=1).then_inc(s_const, 1)
            pool.wait_ge(s_const, 11)
            nc.gpsimd.affine_select(out=group_mask[:], in_=group_mask[:], compare_op=ALU.is_ge, fill=0.0,
                                    base=NTAB - 1, pattern=[[NTAB, BPG]], channel_multiplier=-1
                                    ).then_inc(s_const, 1)

            def gather(tile, parity, earlier):
                if not isinstance(earlier, int) or earlier > 0:
                    pool.wait_ge(s_sw[parity], 16 * earlier)
                nc.gpsimd.tensor_copy(idx[parity][:], ids[:, tile, :]).then_inc(s_idx, 1)
                pool.wait_ge(s_idx, tile + 1)
                pool.sem_inc(s_begun, 1)
                for u in range(4):
                    for n in range(TAB0[u], TAB0[u + 1]):
                        nc.gpsimd.indirect_dma_start(
                            emb[parity][:, n * D:(n + 1) * D], None, tables[n],
                            bass.IndirectOffsetOnAxis(ap=idx[parity][:, n:n + 1], axis=0),
                        ).then_inc(s_gat[parity][u], 16)

            pool.wait_ge(s_ids, 16)
            gather(0, 0, 0)
            gather(1, 1, 0)
            with pool.Fori(1, NTILE // 2) as h:
                gather(2 * h, 0, h)
                gather(2 * h + 1, 1, h)

        @block.tensor
        def _(pe):
            mm, tr = nc.tensor.matmul, nc.tensor.transpose

            pe.wait_ge(s_const, 12)
            pe.wait_ge(s_ld["ws"], 16)
            mm(ps_ab[0][:, 0:D], mean_e[:], ws[:], start=True, stop=True).then_inc(s_p["wsmean"], 1)
            pe.wait_ge(s_ld["wsi"], 16)
            mm(ps_ab[1][0:PROJ, 0:NTAB], mean_p[:], wsi[:], start=True, stop=True).then_inc(s_p["wsimean"], 1)
            pe.wait_ge(s_ld["wd"], 16)
            mm(ps_y[:, 0, 0:D_DENSE], mean_e[:], wd, start=True, stop=True).then_inc(s_p["wdmean"], 1)
            pe.wait_ge(s_v["wc"], 1)
            mm(ps_ab[0][:, 0:2 * D], wc2, wc2, start=True, stop=True).then_inc(s_p["g"], 1)
            pe.wait_ge(s_v["wsi"], 1)
            tr(ps_ab[1][0:GROWS, 0:PROJ], wsc[:].rearrange("p j n -> p (j n)"),
               ident[0:PROJ, 0:PROJ]).then_inc(s_p["wsit"], 1)
            pe.wait_ge(s_v["wd"], 1)
            for k in range(2):
                last = tr(ps_y[:, 1, k * P:(k + 1) * P], wd[:, k * P:(k + 1) * P], ident[:])
            last.then_inc(s_p["wdt"], 1)
            pe.wait_ge(s_v["g"], 1)
            tr(ps_ab[0][:, 0:P], wg2, ident[:]).then_inc(s_p["wpt"], 1)
            pe.wait_ge(s_v["wsct"], 1)
            mm(ps_ab[1][:, 0:PROJ], ones[0:NTAB, :], wsct[0:NTAB, :], start=True, stop=True
               ).then_inc(s_p["sc"], 1)
            pe.wait_ge(s_v["bias"], 1)
            tr(ps_ab[1][0:PROJ, 0:P], bias_y[:], ident[:]).then_inc(s_p["biast"], 1)
            pe.wait_ge(s_ld["dense"], 16)
            for n in range(2 * NSUPER):
                kc, s = n % 2, n // 2
                if n >= 2:
                    pe.wait_ge(s_a["dense_t"], n - 1)
                bank = (ps_tr, ps_gm)[n % 2]
                for t in range(TPS):
                    last = tr(bank[:, t * P:(t + 1) * P], dense[:, TPS * s + t, kc * P:(kc + 1) * P], ident[:])
                last.then_inc(s_p["dense_t"], 1)
            pe.wait_ge(s_a["dense_t"], 2 * NSUPER)
            pe.wait_ge(s_a["wdt"], 1)
            pe.wait_ge(s_v["wp"], 1)
            pe.wait_ge(s_v["bias3"], 1)
            for s in range(NSUPER):
                for kc in range(2):
                    last = mm(x_banks[s], wdt[:, kc, :], super_of(dense_t[:, kc], s), start=(kc == 0), stop=(kc == 1))
                last.then_inc(s_p["x"], 1)
            for s in range(NSUPER):
                pe.wait_ge(s_a["xsq"], s + 1)
                mm(var_banks[s], mean_e[:], super_of(x_sq, s), start=True, stop=True).then_inc(s_p["xvar"], 1)
            pe.wait_ge(s_ld["wl"], 16)
            pe.wait_ge(s_v["xc"], NSUPER)
            for h in range(2):
                for c in range(4):
                    last = mm(ps_ab[h][:, 0:NPAIR // 2], mean_o[:],
                              wl[:, c, h * (NPAIR // 2):(h + 1) * (NPAIR // 2)], start=(c == 0), stop=(c == 3))
                last.then_inc(s_p["wlmean"], 1)
            pe.wait_ge(s_ld["gsi"], 32)
            pe.wait_ge(s_v["xvar"], NSUPER)
            mm(ps_rf[:, 0:2 * PROJ], ones[0:1, :], gsi_row[:], start=True, stop=True).then_inc(s_p["gb"], 1)

            def sum_of_x():
                pe.wait_ge(s_v["x"], 1)
                for s in range(NSUPER):
                    if s >= 2:
                        pe.wait_ge(s_a["sx"], s - 1)
                    mm(ps_y[0:1, s % 2, :], ones[:, 0:1], super_of(xt[:], s), start=True, stop=True
                       ).then_inc(s_p["sx"], 1)

            def front_transpose(H, k):
                f = k + LEAD
                par, u = (f // UPT) % 2, f % UPT
                pe.wait_ge(s_gat[par][u], 16 * (TAB0[u + 1] - TAB0[u]) * (H + (f // UPP + 1)))
                if f > 0:
                    pe.wait_ge(s_et, UPP * H + f)
                for m in range(PAIRS[u]):
                    c0 = (TAB0[u] + 2 * m) * D
                    last = tr(ps_tr[:, m * P:(m + 1) * P], emb[par][:, c0:c0 + P], ident[:])
                last.then_inc(s_tr, 1)

            def front_g(H, k):
                f = k + LEAD
                pe.wait_ge(s_et, UPP * H + (f + 1))
                if f > 0:
                    pe.wait_ge(s_gmr, UPP * H + f)
                for m in range(PAIRS[f % UPT]):
                    last = mm(ps_gm[:, m * P:(m + 1) * P], emb_t[f % 2][:, m * P:(m + 1) * P], gbd[:],
                              start=True, stop=True)
                last.then_inc(s_gm, 1)

            def over_tables(H, k):
                u = k % UPT
                pe.wait_ge(s_xl[u], 32 * H + 16 * (k // UPT + 1))
                if k >= 1:
                    pe.wait_ge(s_qt, UPP * H + k)
                for g in range(4):
                    last = mm(ps_q[:, g * P:(g + 1) * P], xe[u][:, g * P:(g + 1) * P],
                              wbd[:].rearrange("r j p -> r (j p)"), start=True, stop=True)
                last.then_inc(s_q, 1)

            def features(H, k):
                if k >= 1:
                    pe.wait_ge(s_sq, UPP * H + k)
                for a_ in range(2):
                    mm(ps_y[:, a_, :], bias_t[:], select[:].rearrange("k b p -> k (b p)"), start=True, stop=False)
                    if a_ == 0:
                        pe.wait_ge(s_qt, UPP * H + (k + 1))
                    last = mm(ps_y[:, a_, :], wp[a_][:], qt[k % 2][:], start=False, stop=True)
                last.then_inc(s_y, 1)

            def gram_product(H, k):
                pe.wait_ge(s_m, UPP * H + (k + 1))
                if k >= 1:
                    pe.wait_ge(s_g2, UPP * H + k)
                for a_ in range(2):
                    for g in range(4):
                        for j in range(BPG):
                            last = mm(ps_r[PROJ * j:PROJ * (j + 1), 2 * g + a_, :], cen[k % 2][:, a_, g, j, :],
                                      mov[k % 2][:, a_, g, j, :], start=True, stop=True,
                                      tile_position=(0, PROJ * j))
                last.then_inc(s_gr, 1)

            def step(H, k):
                if unit(H, k + LEAD):
                    front_transpose(H, k)
                if unit(H, k + 1):
                    over_tables(H, k + 1)
                if unit(H, k - 2):
                    gram_product(H, k - 2)
                if unit(H, k + LEAD):
                    front_g(H, k)
                if unit(H, k):
                    features(H, k)

            def outputs(S, c):
                if c == 0:
                    pe.wait_ge(s_fr, 16 * READS * (S + 1))
                    pe.wait_ge(s_yc, S + 1)
                if c >= 2:
                    pe.wait_ge(s_zc, 4 * S + (c - 1))
                for n in range(NFULL):
                    mm(ps_ab[c % 2][:], wl_t[:, n, c * P:(c + 1) * P], f_sb[:, n, :], start=(n == 0), stop=False)
                mm(ps_ab[c % 2][:], wl_t[0:LASTK, NFULL, c * P:(c + 1) * P], f_last[:, S, :],
                   start=False, stop=True).then_inc(s_z, 1)

            def square_sum(S):
                pe.wait_ge(s_zc, 4 * S + 4)
                for c in range(4):
                    last = mm(ps_ab[0][:], mean_o[:], z_sq[:, c, :], start=(c == 0), stop=(c == 3))
                last.then_inc(s_ss, 1)

            def layer1_dense(S, h):
                if h == 1:
                    pe.wait_ge(s_zv, S + 1)
                if h >= 2:
                    pe.wait_ge(s_h1r, 4 * S + (h - 1))
                for kc in range(2):
                    mm(ps_ab[1 - h % 2][:], w1[:, 3 + kc, h * P:(h + 1) * P], super_of(dense_t[:, kc], S),
                       start=(kc == 0), stop=False)

            def layer1_z(S, h):
                pe.wait_ge(s_zs, S + 1)
                for kc in range(3):
                    last = mm(ps_ab[1 - h % 2][:], w1[:, kc, h * P:(h + 1) * P], z_sb[:, kc, :],
                              start=False, stop=(kc == 2))
                last.then_inc(s_h1, 1)

            def layer2(S, h):
                for kc in range(4):
                    if h == 0 or kc == 0:
                        pe.wait_ge(s_h1r, 4 * S + max(kc + 1, h + 3))
                    last = mm(ps_ab[1 - h][:], w2[:, kc, h * P:(h + 1) * P], h1_sb[:, kc, :],
                              start=(kc == 0), stop=(kc == 3))
                last.then_inc(s_h2, 1)

            def layer3(S):
                for kc in range(2):
                    pe.wait_ge(s_h2r, 2 * S + (kc + 1))
                    last = mm(ps_ab[1][0:1, :], w3[:, kc:kc + 1], h2_sb[:, kc, :], start=(kc == 0), stop=(kc == 1))
                last.then_inc(s_yo, 1)

            def tail(S, part):
                if part < 4:
                    outputs(S, part)
                elif part == 4:
                    square_sum(S)
                elif part < 7:
                    layer1_dense(S, part - 5)
                elif part == 7:
                    layer1_z(S, 0)
                    layer1_z(S, 1)
                elif part < 10:
                    layer1_dense(S, part - 6)
                    layer1_z(S, part - 6)
                elif part == 10:
                    layer2(S, 0)
                else:
                    layer2(S, 1)
                    layer3(S)

            for k in range(-LEAD, 0):
                front_transpose(0, k)
                front_g(0, k)
            sum_of_x()
            pe.wait_ge(s_a["sx"], NSUPER)
            pe.wait_ge(s_v["gb"], 1)
            pe.wait_ge(s_v["wbd"], 1)
            over_tables(0, 0)
            for k in range(4):
                step(0, k)
            with pe.Fori(0, 2) as H:
                for k in range(4, 12):
                    step(H, k)
            pe.wait_ge(s_v["wlrows"], 4)
            for n in range(READS):
                width = P if n < NFULL else LASTK
                if n >= 2:
                    pe.wait_ge(s_a["wlt"], n - 1)
                for c in range(4):
                    last = tr(ps_ab[n % 2][0:width, c * P:(c + 1) * P], wl_x[:, c, n * P:n * P + width], ident[:])
                last.then_inc(s_p["wlt"], 1)
            pe.wait_ge(s_a["wlt"], READS)
            pe.wait_ge(s_ld["w1"], 32)
            pe.wait_ge(s_ld["bl"], 16)
            for h in range(4):
                for kc in range(3):
                    last = mm(ps_ab[1][:, h:h + 1], w1[:, kc, h * P:(h + 1) * P], bl[:, kc:kc + 1],
                              start=(kc == 0), stop=(kc == 2))
            last.then_inc(s_p["b1"], 1)
            pe.wait_ge(s_ld["w2"], 16)
            pe.wait_ge(s_ld["w3"], 16)
            pe.wait_ge(s_v["b1"], 1)
            with pe.Fori(0, 2) as T:
                for k in range(4, 20):
                    step(2 * T + 2, k)
                    if k >= 8:
                        tail(T, k - 8)
            for k in range(4, 20):
                step(6, k)
                if k >= 8:
                    tail(2, k - 8)
            for part in range(12):
                tail(3, part)

        @block.scalar
        def _(act):
            cp = nc.scalar.copy

            act.wait_ge(s_p["wdt"], 1)
            cp(wdt[:].rearrange("p k e -> p (k e)"), ps_y[:, 1, 0:2 * P]).then_inc(s_a["wdt"], 1)
            for n in range(2 * NSUPER):
                kc, s = n % 2, n // 2
                act.wait_ge(s_p["dense_t"], n + 1)
                cp(super_of(dense_t[:, kc], s).rearrange("k j g -> k g j"),
                   (ps_tr, ps_gm)[n % 2][:].rearrange("k (g j) -> k g j", j=BPG)).then_inc(s_a["dense_t"], 1)
            for s in range(NSUPER):
                act.wait_ge(s_v["xc"], s + 1)
                nc.scalar.activation(super_of(x_sq, s), super_of(xt[:], s), ACT.Square).then_inc(s_a["xsq"], 1)
            act.wait_ge(s_v["xrr"], 1)
            nc.scalar.activation(x_rs, x_rr, ACT.Sqrt).then_inc(s_a["xrs"], 1)

            def sum_of_x():
                for s in range(NSUPER):
                    act.wait_ge(s_p["sx"], s + 1)
                    cp(f_last[2 * PROJ:LASTK, s, :], ps_y[0:1, s % 2, :]).then_inc(s_a["sx"], 1)

            def front_copy(H, k):
                f = k + LEAD
                w = PAIRS[f % UPT] * P
                act.wait_ge(s_tr, UPP * H + (f + 1))
                if f >= 2:
                    act.wait_ge(s_gm, UPP * H + (f - 1))
                cp(emb_t[f % 2][:, 0:w], ps_tr[:, 0:w]).then_inc(s_et, 1)

            def front_sqrt(H, k):
                f = k + LEAD
                if f % UPT == UPT - 1:
                    act.wait_ge(s_vbr, 2 * H + (f // UPT + 1))
                    nc.scalar.activation(rs_b[:], var_r[:], ACT.Sqrt).then_inc(s_rb, 1)

            def q_copy(H, k):
                act.wait_ge(s_q, UPP * H + (k + 1))
                if k >= 2:
                    act.wait_ge(s_y, UPP * H + (k - 1))
                cp(qt[k % 2][:], ps_q[:]).then_inc(s_qt, 1)

            def feature_copy(H, k):
                act.wait_ge(s_y, UPP * H + (k + 1))
                if k >= 2:
                    act.wait_ge(s_gr, UPP * H + (k - 1))
                both = ps_y[:].rearrange("e a (g j p) -> e a g j p", j=BPG, p=PROJ)
                cp(cen[k % 2][:], both).then_inc(s_c, 1)
                if k >= 1:
                    act.wait_ge(s_v2, UPP * H + k)
                nc.scalar.activation(sq[:], both, ACT.Square).then_inc(s_sq, 1)

            def feature_sqrt(H, k):
                act.wait_ge(s_r2, UPP * H + (k + 1))
                nc.scalar.activation(mov[k % 2][:, :, :, :, QN - 1], r2[:], ACT.Sqrt).then_inc(s_rs, 1)

            def gram_copy(H, k, written=None):
                act.wait_ge(s_gr, UPP * H + (k + 1))
                if written is not None:
                    act.wait_ge(s_fw, 16 * WRITES * written)
                g0 = (H * (UPP * GPU) + k * GPU) % (2 * GPS)
                cp(gram[:, :, bass.ds(g0, GPU)], ps_r.rearrange("p g q -> p q g")).then_inc(s_g2, 1)

            def step(H, k, written=None, tail_part=None):
                if unit(H, k - 1) and (k >= 1):
                    feature_copy(H, k - 1)
                if unit(H, k + LEAD):
                    front_copy(H, k)
                if unit(H, k + 1):
                    q_copy(H, k + 1)
                if tail_part is not None:
                    tail(*tail_part)
                if unit(H, k - 2) and k >= 2:
                    gram_copy(H, k - 2, written)
                if unit(H, k - 1) and k >= 1:
                    feature_sqrt(H, k - 1)
                if unit(H, k + LEAD):
                    front_sqrt(H, k)

            def tail(S, part):
                if part < 4:
                    act.wait_ge(s_z, 4 * S + (part + 1))
                    if part < 3:
                        nc.scalar.activation(z_c[:, part, :], ps_ab[part % 2][:], ACT.Identity,
                                             bias=const_z[:, part:part + 1])
                    nc.scalar.activation(z_sq[:, part, :], ps_ab[part % 2][:], ACT.Square,
                                         bias=const_z[:, part:part + 1]).then_inc(s_zc, 1)
                elif part == 5:
                    act.wait_ge(s_zr, S + 1)
                    nc.scalar.activation(rz_sb, rz_v, ACT.Sqrt).then_inc(s_rz, 1)
                elif 7 <= part < 10:
                    for h in ((0, 1), (2,), (3,))[part - 7]:
                        act.wait_ge(s_h1, 4 * S + (h + 1))
                        nc.scalar.activation(h1_sb[:, h, :], ps_ab[1 - h % 2][:], ACT.Relu,
                                             bias=b1x[:, h:h + 1]).then_inc(s_h1r, 1)
                elif part >= 10:
                    h = part - 10
                    act.wait_ge(s_h2, 2 * S + (h + 1))
                    nc.scalar.activation(h2_sb[:, h, :], ps_ab[1 - h][:], ACT.Relu,
                                         bias=b2[:, h:h + 1]).then_inc(s_h2r, 1)
                if part == 11:
                    act.wait_ge(s_yo, S + 1)
                    act.wait_ge(s_out, 16 * (S + 1))
                    cp(y_sb.rearrange("o (g j) -> o g j", j=BPG),
                       ps_ab[1][0:1, :].rearrange("o (j g) -> o g j", j=BPG)).then_inc(s_yc, 1)
                    act.wait_ge(s_yc, S + 2)
                    act.dma_start(out[bass.ds(S * SUPER, SUPER), :].rearrange("(o b) c -> o (b c)", o=1), y_sb
                                  ).then_inc(s_out, 16)

            for k in range(-LEAD, 0):
                front_copy(0, k)
                front_sqrt(0, k)
            sum_of_x()
            q_copy(0, 0)
            for k in range(4):
                step(0, k)
            with act.Fori(0, 2) as H:
                for k in range(4, 12):
                    step(H, k)
            for n in range(READS):
                width = P if n < NFULL else LASTK
                act.wait_ge(s_p["wlt"], n + 1)
                cp(wl_t[0:width, n, :], ps_ab[n % 2][0:width, :]).then_inc(s_a["wlt"], 1)
            act.wait_ge(s_ld["b2"], 16)
            act.wait_ge(s_v["b1"], 1)
            act.sem_inc(s_out, 16)
            act.sem_inc(s_yc, 1)
            with act.Fori(0, 2) as T:
                for k in range(4, 20):
                    step(2 * T + 2, k, T + 1 if k == 18 else None, (T, k - 9) if k >= 9 else None)
                tail(T, 11)
            for k in range(4, 20):
                step(6, k, None, (2, k - 9) if k >= 9 else None)
            tail(2, 11)
            for part in range(12):
                tail(3, part)
            act.wait_ge(s_out, 16 * (NSUPER + 1))

        @block.vector
        def _(dve):
            tt, ts = nc.vector.tensor_tensor, nc.vector.tensor_scalar
            chain = [0]

            def link(ins):
                chain[0] += 1
                ins.then_inc(s_chain, 1)
                dve.wait_ge(s_chain, chain[0])

            dve.wait_ge(s_p["wsmean"], 1)
            for h in range(2):
                last = tt(wc2[:, h * D:(h + 1) * D], ws[:], ps_ab[0][:, 0:D], ALU.subtract)
            last.then_inc(s_v["wc"], 1)
            dve.wait_ge(s_p["wsimean"], 1)
            for j in range(BPG):
                last = tt(wsc[:, j, :], wsi[:], ps_ab[1][0:PROJ, 0:NTAB], ALU.subtract)
            last.then_inc(s_v["wsi"], 1)
            dve.wait_ge(s_p["wdmean"], 1)
            tt(wd, wd, ps_y[:, 0, 0:D_DENSE], ALU.subtract).then_inc(s_v["wd"], 1)
            dve.wait_ge(s_p["g"], 1)
            dve.wait_ge(s_const, 12)
            dve.wait_ge(s_ld["vec"], 64)
            dve.wait_ge(s_v["wc"], 1)
            for h in range(2):
                r = slice(h * D, (h + 1) * D)
                ts(gbd[r, r], ps_ab[0][r, r], 1.0 / E_DIM, None, ALU.mult)
            ts(wg2, wc2, vec[:, 0:1], None, ALU.mult).then_inc(s_v["g"], 1)
            dve.wait_ge(s_p["wsit"], 1)
            nc.vector.tensor_copy(wsct[:], ps_ab[1][0:GROWS, 0:PROJ]).then_inc(s_v["wsct"], 1)
            dve.wait_ge(s_v["wsct"], 1)
            for j in range(BPG):
                last = ts(wbd[:, j, :], wsct[:], group_mask[:, j:j + 1], None, ALU.mult)
            last.then_inc(s_v["wbd"], 1)
            dve.wait_ge(s_p["wpt"], 1)
            nc.vector.tensor_copy(wp[0][0:D, :], ps_ab[0][0:D, 0:P])
            nc.vector.tensor_copy(wp[1][D:2 * D, :], ps_ab[0][D:2 * D, 0:P]).then_inc(s_v["wp"], 1)
            dve.wait_ge(s_p["sc"], 1)
            ts(bias_y[:], ps_ab[1][:, 0:PROJ], vec[:, 1:2], None, ALU.mult).then_inc(s_v["bias"], 1)
            for q in range(3):
                r = slice(q * PROJ, (q + 1) * PROJ)
                nc.vector.tensor_copy(select[r], ident[r, r].unsqueeze(1).to_broadcast([PROJ, 512 // PROJ, PROJ]))
            dve.wait_ge(s_p["biast"], 1)
            link(nc.vector.tensor_copy(bias_h[:], ps_ab[1][0:PROJ, 0:P]))
            nc.vector.tensor_copy(bias_t[0:PROJ, :], bias_h[:])
            link(tt(bias_r[:, 0, :], ps_ab[1][0:PROJ, 0:P], bias_h[:], ALU.subtract))
            link(nc.vector.tensor_copy(bias_h[:], bias_r[:, 0, :]))
            nc.vector.tensor_copy(bias_t[PROJ:2 * PROJ, :], bias_h[:])
            link(tt(bias_r[:, 1, :], bias_r[:, 0, :], bias_h[:], ALU.subtract))
            nc.vector.tensor_copy(bias_t[2 * PROJ:3 * PROJ, :], bias_r[:, 1, :]).then_inc(s_v["bias3"], 1)
            for s in range(NSUPER):
                dve.wait_ge(s_p["x"], s + 1)
                nc.vector.tensor_copy(super_of(xt[:], s), x_banks[s].rearrange("e (j g) -> e j g", j=BPG)).then_inc(s_v["xc"], 1)
            for s in range(NSUPER):
                dve.wait_ge(s_p["xvar"], s + 1)
                ts(super_of(x_rs, s), var_banks[s].rearrange("e (j g) -> e j g", j=BPG), EPS, None, ALU.add).then_inc(s_v["xvar"], 1)
            dve.wait_ge(s_v["xvar"], NSUPER)
            nc.vector.reciprocal(x_rr, x_rs).then_inc(s_v["xrr"], 1)
            for h in range(2):
                dve.wait_ge(s_p["wlmean"], h + 1)
                for c in range(4):
                    r = slice(h * (NPAIR // 2), (h + 1) * (NPAIR // 2))
                    last = tt(wl[:, c, r], wl[:, c, r], ps_ab[h][:, 0:NPAIR // 2], ALU.subtract)
            last.then_inc(s_v["wlsub"], 1)
            dve.wait_ge(s_p["gb"], 1)
            nc.vector.tensor_copy(gb[:], ps_rf[:, 0:2 * PROJ]).then_inc(s_v["gb"], 1)
            dve.wait_ge(s_a["xrs"], 1)
            link(nc.vector.scalar_tensor_tensor(out=xt[:], in0=xt[:], scalar=vec[:, 2:3], in1=x_rs,
                                                op0=ALU.mult, op1=ALU.mult))
            ts(xt[:], xt[:], vec[:, 3:4], None, ALU.add).then_inc(s_v["x"], 1)

            def low_rows():
                link(nc.vector.memset(wl_low[:], 0.0))
                dve.wait_ge(s_v["wlsub"], 1)
                for p in range(PROJ):
                    r0 = p * (p + 1) // 2
                    last = nc.vector.tensor_copy(wl_low[:, :, 0:p + 1, p], wl[:, :, r0:r0 + p + 1])
                link(last)
                dve.wait_ge(s_v["gb"], 1)

            def weight_rows(c):
                low_c = wl_low[:, c]
                gsi, bsi = gb[:, 0:PROJ], gb[:, PROJ:]
                over_q = [P, PROJ + 1, PROJ]
                link(tt(prep_tmp[:], low_c, bsi.unsqueeze(1).to_broadcast(over_q), ALU.mult))
                link(nc.vector.tensor_reduce(small[:, 0, :], prep_tmp[:], AX.X, ALU.add))
                link(tt(prep_tmp[:, 0:PROJ, :], low_c[:, 1:, :],
                        bsi.unsqueeze(2).to_broadcast([P, PROJ, PROJ]), ALU.mult))
                link(nc.vector.tensor_reduce(small[:, 1, 0:PROJ],
                                             prep_tmp[:, 0:PROJ, :].rearrange("o q p -> o p q"), AX.X, ALU.add))
                link(tt(small[:, 2, 0:PROJ], small[:, 0, 1:], bsi, ALU.mult))
                link(nc.vector.tensor_reduce(const_z[:, c:c + 1], small[:, 2, 0:PROJ], AX.X, ALU.add))
                link(ts(const_z[:, c:c + 1], const_z[:, c:c + 1], float(E_DIM), None, ALU.mult))
                link(tt(small[:, 3, 0:PROJ], small[:, 0, 1:], small[:, 1, 0:PROJ], ALU.add))
                r = NFULL * P
                tt(wl_x[:, c, r + PROJ:r + 2 * PROJ], small[:, 3, 0:PROJ], gsi, ALU.mult)
                nc.vector.tensor_copy(wl_x[:, c, r + 2 * PROJ:r + LASTK], small[:, 0, 0:1])
                link(tt(low_c, low_c, gsi.unsqueeze(1).to_broadcast(over_q), ALU.mult))
                nc.vector.tensor_copy(wl_x[:, c, r:r + PROJ], low_c[:, 0, :])
                for row, q0, nq, p0, np_ in BLOCKS:
                    last = tt(wl_x[:, c, row:row + nq * np_].rearrange("o (q p) -> o q p", q=nq),
                              low_c[:, 1 + q0:1 + q0 + nq, p0:p0 + np_],
                              gsi[:, q0:q0 + nq].unsqueeze(2).to_broadcast([P, nq, np_]), ALU.mult)
                last.then_inc(s_v["wlrows"], 1)

            def front_var(H, k):
                f = k + LEAD
                par, u = (f // UPT) % 2, f % UPT
                w = PAIRS[u] * P
                dve.wait_ge(s_gm, UPP * H + (f + 1))
                tt(prod[f % 2][:, 0:w], ps_gm[:, 0:w], emb[par][:, TAB0[u] * D:TAB0[u] * D + w], ALU.mult
                   ).then_inc(s_gmr, 1)
                dve.wait_ge(s_gmr, UPP * H + (f + 1))
                nc.vector.tensor_reduce(var_b[:, TAB0[u]:TAB0[u + 1]],
                                        prod[f % 2][:, 0:w].rearrange("b (n d) -> b n d", d=D), AX.X, ALU.add
                                        ).then_inc(s_vb, 1)

            def front_scale(H, k):
                f = k + LEAD
                if f % UPT == UPT - 1:
                    c = f // UPT
                    dve.wait_ge(s_vb, UPP * H + (f + 1))
                    ts(var_e[:], var_b[:], EPS, None, ALU.add).then_inc(s_vbe, 1)
                    dve.wait_ge(s_vbe, 2 * H + (c + 1))
                    nc.vector.reciprocal(var_r[:], var_e[:]).then_inc(s_vbr, 1)
                    dve.wait_ge(s_rb, 2 * H + (c + 1))
                    e = emb[c % 2][:].rearrange("b (n d) -> b n d", d=D)
                    tt(e, e, rs_b[:].unsqueeze(2).to_broadcast([P, NTAB, D]), ALU.mult).then_inc(s_sc, 1)

            def moving(H, k):
                p, n = k % 2, UPP * H + (k + 1)
                dve.wait_ge(s_sq, n)
                nc.vector.tensor_reduce(v2[:], sq[:].rearrange("e a g j p -> e (a g j) p"), AX.X, ALU.add
                                        ).then_inc(s_v2, 1)
                dve.wait_ge(s_v2, n)
                ts(v2e[:], v2[:], 1.0 / PROJ, EPS, ALU.mult, ALU.add).then_inc(s_v2e, 1)
                dve.wait_ge(s_v2e, n)
                nc.vector.reciprocal(r2[:].rearrange("e a g j -> e (a g j)"), v2e[:]).then_inc(s_r2, 1)
                dve.wait_ge(s_r2, n)
                m = mov[p][:].rearrange("e a g j q -> e (a g j) q")
                tt(m[:, :, 0:PROJ], cen[p][:].rearrange("e a g j p -> e (a g j) p"),
                   r2[:].rearrange("e a g j -> e (a g j)").unsqueeze(2).to_broadcast([P, UNIT, PROJ]), ALU.mult)
                dve.wait_ge(s_rs, n)
                x = xt[:, :, bass.ds(H * (UPP * GPU) + k * GPU, GPU)].rearrange("e j (g a) -> e a g j", a=2)
                for a_ in range(2):
                    last = tt(mov[p][:, a_, :, :, PROJ], mov[p][:, a_, :, :, PROJ + 1], x[:, a_], ALU.mult)
                last.then_inc(s_m, 1)

            def step(H, k, tail_part=None):
                if unit(H, k - 1) and k >= 1:
                    moving(H, k - 1)
                if unit(H, k + LEAD):
                    front_var(H, k)
                    front_scale(H, k)
                if tail_part is not None:
                    tail(*tail_part)

            def tail(S, part):
                if part == 4:
                    dve.wait_ge(s_ss, S + 1)
                    ts(rz_sb, ps_ab[0][:], EPS, None, ALU.add).then_inc(s_zv, 1)
                    dve.wait_ge(s_zv, S + 1)
                    nc.vector.reciprocal(rz_v, rz_sb).then_inc(s_zr, 1)
                elif part == 5:
                    dve.wait_ge(s_rz, S + 1)
                    for c in range(3):
                        last = nc.vector.scalar_tensor_tensor(
                            out=z_sb[:, c, :], in0=z_c[:, c, :], scalar=gl[:, c:c + 1], in1=rz_sb,
                            op0=ALU.mult, op1=ALU.mult)
                    last.then_inc(s_zs, 1)

            for k in range(-LEAD, 0):
                front_var(0, k)
                front_scale(0, k)
            for k in range(4):
                step(0, k)
                if k == 0:
                    low_rows()
                else:
                    weight_rows(k - 1)
            weight_rows(3)
            with dve.Fori(0, 2) as H:
                for k in range(4, 12):
                    step(H, k)
            dve.wait_ge(s_p["b1"], 1)
            dve.wait_ge(s_ld["b1"], 16)
            tt(b1x[:], ps_ab[1][:, 0:4], b1[:], ALU.add).then_inc(s_v["b1"], 1)
            dve.wait_ge(s_ld["gl"], 16)
            with dve.Fori(0, 2) as T:
                for k in range(4, 20):
                    step(2 * T + 2, k, (T, k - 9) if k >= 9 else None)
            for k in range(4, 20):
                step(6, k, (2, k - 9) if k >= 9 else None)
            for part in range(12):
                tail(3, part)


_NAMES = (["r_dense_t", "ids"] + [f"tbl_{n}" for n in range(NTAB)]
          + ["W_top1", "b_top1", "W_top2", "b_top2", "W_top3"]
          + [f"L0_rec_{n}" for n in ("Wd", "gd", "bd", "Ws", "gs", "bs", "Wsi", "gsi", "bsi", "Wl", "gl", "bl")])


def kernel(**inputs):
    import numpy as np
    import concourse.bacc as bacc
    from concourse.bass_utils import run_bass_kernel_spmd

    nc = bacc.Bacc("TRN2", target_bir_lowering=False, num_devices=1)
    arrays, args = {}, {}
    for name in _NAMES:
        x = np.ascontiguousarray(inputs[name])
        arrays[f"in_{name}"] = x
        args[name] = nc.dram_tensor(f"in_{name}", x.shape, mybir.dt.from_np(x.dtype), kind="ExternalInput").ap()
    out = nc.dram_tensor("out_y", (ROWS, 1), F32, kind="ExternalOutput").ap()
    interaction_tower(nc, args, out)
    r = run_bass_kernel_spmd(nc, [arrays], core_ids=[0])
    return r.results[0]["out_y"]
```

```python
from contextlib import ExitStack

import concourse.bass as bass
from concourse import mybir

F32 = mybir.dt.float32
BF16 = mybir.dt.bfloat16
F32R = mybir.dt.float32r
I32 = mybir.dt.int32
ALU = mybir.AluOpType
ACT = mybir.ActivationFunctionType
AX = mybir.AxisListType

ROWS = 2048
NTAB, D = 26, 64
E_DIM, PROJ = 128, 32
D_DENSE = 256
MAXD, USED = 512, 384
H1, H2 = 512, 256
NPAIR = (PROJ + 1) * PROJ // 2
EPS = 1e-5
P = 128

TILE = 128
NTILE = ROWS // TILE
UNIT = 32
UPT = TILE // UNIT
SUPER = 512
TPS = SUPER // TILE
NSUPER = ROWS // SUPER
BPG = 4
GROWS = BPG * NTAB
GPU = UNIT // BPG
GPS = SUPER // BPG
UPS = TPS * UPT
UPP = 2 * UPT
NUNIT = ROWS // UNIT
WHOLE = (14, 16, 17)
SPLITS = UPS - len(WHOLE)
LEAD = 6

PAIRS = [4, 3, 3, 3]
TAB0 = [0, 8, 14, 20, 26]
QN = PROJ + 2
GRAM_ROWS = QN * PROJ + 1

CHUNKS = [[(8 * h, 8, 16, 16)] for h in range(2)]
CHUNKS += [[(16 * h, 8, 16 * h + 8, 8) for h in range(2)]]
CHUNKS += [[(0, 7, 1, 7), (8, 7, 9, 7), (24, 4, 28, 4), (24, 3, 25, 3)]]
CHUNKS += [[(16, 7, 17, 7), (28, 3, 29, 3), (PROJ, 2, 0, PROJ)]]
NCHUNK = len(CHUNKS)
CH = [sum(b[1] * b[3] for b in chunk) + (chunk == CHUNKS[-1]) for chunk in CHUNKS]
ROW0 = [sum(CH[:n]) for n in range(NCHUNK)]
NROW = sum(CH)
SXROW = NROW - 1
XROW = SXROW - 2 * PROJ
BLOCKS = []
for chunk, row0 in zip(CHUNKS, ROW0):
    for q0, nq, p0, np_ in chunk:
        if q0 < PROJ:
            BLOCKS.append((row0, q0, nq, p0, np_))
        row0 += nq * np_
WRITTEN = [(0, 16, 0, PROJ), (16, 16, 16, 16), (PROJ, 2, 0, PROJ)]
SX_D = QN * PROJ
WRITES = BPG * len(WRITTEN)
READS = sum(len(chunk) for chunk in CHUNKS)
LINKS = 9


def interaction_tower(nc, a, out):
    tables = [a[f"tbl_{n}"] for n in range(NTAB)]
    scaled_d = nc.dram_tensor("scaled_d", (NTILE, TILE * NTAB, D), F32, kind="Internal").ap()
    gram_d = nc.dram_tensor("gram_d", (NSUPER, GRAM_ROWS, BPG, GPS), F32, kind="Internal").ap()

    with ExitStack() as ctx:
        ctx.enter_context(nc.allow_non_contiguous_dma(reason="bias vectors, once"))

        def sb(name, shape, dt=F32):
            return ctx.enter_context(nc.sbuf_tensor(name, shape, dt))

        def pb(name, shape):
            return ctx.enter_context(nc.psum_tensor(name, shape, F32))

        def sem(name):
            return ctx.enter_context(nc.semaphore(name))

        ps_tr = pb("ps_tr", [P, 512])
        ps_gm = pb("ps_gm", [P, 512])
        ps_q = pb("ps_q", [P, 512])
        ps_y = pb("ps_y", [P, 2, 512])
        ps_rf = pb("ps_r", [P, 512])
        ps_r = ps_rf[:, 0:GPU * QN].rearrange("p (g q) -> p g q", q=QN)
        ps_ab = [pb("ps_a", [P, 512]), pb("ps_b", [P, 512])]

        ident = sb("ident", [P, P])
        ones = sb("ones", [P, P])
        mean_e = sb("mean_e", [P, P])
        mean_o = sb("mean_o", [P, P])
        mean_p = sb("mean_p", [PROJ, PROJ])
        group_mask = sb("group_mask", [GROWS, BPG])

        ws = sb("ws", [P, D])
        wsi = sb("wsi", [PROJ, NTAB])
        vec = sb("vec", [P, 4])
        gsi_row = sb("gsi_row", [1, 2 * PROJ])
        w1 = sb("w1", [P, 5, H1])
        w2 = sb("w2", [P, 4, H2])
        w3 = sb("w3", [P, 2])
        b1 = sb("b1", [P, 4])
        b2 = sb("b2", [P, 2])
        gl = sb("gl", [P, 3])
        bl = sb("bl", [P, 3])
        wl = sb("wl", [P, 4, NPAIR])

        gbd = sb("gbd", [P, P])
        wp = [sb("wp0", [P, E_DIM]), sb("wp1", [P, E_DIM])]
        w_high = sb("w_high", [P, E_DIM], F32R)
        w_low = sb("w_low", [P, E_DIM], F32R)
        wsc = sb("wsc", [PROJ, BPG, NTAB])
        wsct = sb("wsct", [GROWS, PROJ])
        wbd = sb("wbd", [GROWS, BPG, PROJ])
        bias_y = sb("bias_y", [P, PROJ])
        bias_h = sb("bias_h", [PROJ, E_DIM], BF16)
        bias_t = sb("bias_t", [3 * PROJ, E_DIM], BF16)
        select = sb("select", [3 * PROJ, 512 // PROJ, PROJ], BF16)
        wdt = sb("wdt", [P, 2, E_DIM])
        gb = sb("gb", [P, 2 * PROJ])
        wl_low = sb("wl_low", [P, 4, PROJ + 1, PROJ])
        wl_x = sb("wl_x", [P, 4, NROW])
        wl_t = sb("wl_t", [P, NCHUNK, MAXD])
        const_z = sb("const_z", [P, 4])
        b1x = sb("b1x", [P, 4])
        small = sb("small", [P, 4, PROJ + 1])

        ids = sb("ids", [P, NTILE, NTAB], I32)
        idx = [sb(f"idx{i}", [P, NTAB], I32) for i in range(2)]
        emb = [sb(f"emb{i}", [P, NTAB * D]) for i in range(2)]
        emb_t = [sb(f"emb_t{i}", [P, 512]) for i in range(2)]
        prod = [sb(f"prod{i}", [P, 512]) for i in range(2)]
        var_b = sb("var_b", [P, NTAB])
        var_e = sb("var_e", [P, NTAB])
        var_r = sb("var_r", [P, NTAB])
        rs_b = sb("rs_b", [P, NTAB])
        xe = [sb(f"xe{u}", [GROWS, GPU * D]) for u in range(UPT)]
        qt = [sb(f"qt{i}", [P, 512]) for i in range(2)]
        qs = [sb(f"qs{i}", [P, 2, 512], F32R) for i in range(2)]
        cen = [sb(f"cen{i}", [P, 2, 4, BPG, PROJ]) for i in range(2)]
        sq = sb("sq", [P, 2, 4, BPG, PROJ])
        mov = [sb(f"mov{i}", [P, 2, 4, BPG, QN]) for i in range(2)]
        v2 = sb("v2", [P, UNIT])
        v2e = sb("v2e", [P, UNIT])
        r2 = sb("r2", [P, 2, 4, BPG])
        gram = sb("gram", [P, QN, 2 * GPS])
        f_sb = sb("f_sb", [P, NCHUNK, SUPER])
        y_sb = sb("y_sb", [1, SUPER])
        var_s = sb("var_s", [P, NTILE])
        rec_s = sb("rec_s", [P, NTILE])
        rt_s = sb("rt_s", [P, NTILE])
        dense_t = sb("dense_t", [P, 2, BPG, ROWS // BPG])
        xt = sb("xt", [P, BPG, ROWS // BPG])
        prep_tmp = sb("prep_tmp", [P, PROJ + 1, PROJ])

        ring = gram[:].rearrange("p q g -> p (q g)")
        dense = ring[:, 0:NTILE * D_DENSE].rearrange("p (t k) -> p t k", t=NTILE)
        x_sq = ring[:, 2 * ROWS:3 * ROWS].rearrange("p (j g) -> p j g", j=BPG)
        x_diag = ring[:, 3 * ROWS:4 * ROWS].rearrange("p (n b) -> p n b", n=NTILE)
        spare = ring[:, 4 * ROWS:]
        wd = spare[:, 0:D_DENSE]
        wc2 = spare[:, D_DENSE:D_DENSE + 2 * D]
        wg2 = spare[:, D_DENSE + 2 * D:D_DENSE + 4 * D]
        bias_r = mov[0][:].rearrange("p a g j q -> p (a g j q)")[0:PROJ, 0:2 * E_DIM].rearrange(
            "p (n e) -> p n e", n=2)
        low = wl_low[:].rearrange("p c q k -> p (c q k)")
        z_c = low[:, 0:1536].rearrange("p (c b) -> p c b", c=3)
        z_sq = low[:, 1536:3584].rearrange("p (c b) -> p c b", c=4)
        z_diag = low[:, 3584:4096].rearrange("p (n b) -> p n b", n=TPS)
        old_wl = wl[:].rearrange("p c k -> p (c k)")
        z_sb = old_wl[:, 0:1536].rearrange("p (c b) -> p c b", c=3)
        gg = old_wl[:, 0:PROJ * PROJ].rearrange("p (q k) -> p q k", q=PROJ)
        old_wl_x = wl_x[:].rearrange("p c k -> p (c k)")
        h1_sb = old_wl_x[:, 0:4 * SUPER].rearrange("p (c b) -> p c b", c=4)
        h2_sb = prep_tmp[:].rearrange("p q k -> p (q k)")[:, 0:2 * SUPER].rearrange("p (c b) -> p c b", c=2)

        s_const = sem("const_ready")
        s_ld = {n: sem(f"ld_{n}") for n in ("ws", "wd", "wsi", "vec", "gsi", "w1", "w2", "w3", "b1", "b2",
                                            "gl", "bl", "wl", "dense")}
        s_ids = sem("ids_loaded")
        s_idx = sem("tile_ids_ready")
        s_begun = sem("gather_tiles_begun")
        s_gat = [[sem(f"gathered{i}_{u}") for u in range(4)] for i in range(2)]
        s_sw = [[sem(f"scaled_written{i}_{h}") for h in range(2)] for i in range(2)]
        s_xl = [sem(f"unit_loaded{u}") for u in range(UPT)]
        s_fw = sem("gram_written")
        s_fr = sem("gram_read_back")
        s_sxw = sem("sum_of_x_written")
        s_out = sem("out_written")
        s_p = {n: sem(f"prep_p_{n}") for n in ("wsmean", "wsimean", "wdmean", "g", "wsit", "wdt", "wpt", "sc", "biast",
                                               "dense_t", "x", "xvar", "xbc", "wlmean", "gb", "sx", "wlt", "b1")}
        s_a = {n: sem(f"prep_a_{n}") for n in ("wdt", "dense_t", "xsq", "xrt", "x", "sx", "wlt")}
        s_v = {n: sem(f"prep_v_{n}") for n in ("low", "wc", "wsi", "wd", "g", "wsct", "wbd", "wp", "bias", "bias3", "xc", "xvar",
                                               "xrr", "xdiag", "x", "wlsub", "gb", "wlrows", "b1")}
        s_tr = sem("emb_transposed")
        s_gm = sem("emb_g_ready")
        s_q = sem("q_ready")
        s_y = sem("y_ready")
        s_gr = sem("gram_ready")
        s_z = sem("z_ready")
        s_ss = sem("z_square_sum_ready")
        s_zb = sem("z_r_on_all_partitions")
        s_h1 = sem("h1_ready")
        s_h2 = sem("h2_ready")
        s_yo = sem("y_out_ready")
        s_et = sem("emb_t_copied")
        s_qt = sem("qt_copied")
        s_ql = sem("q_low_ready")
        s_sq = sem("squared")
        s_rs = sem("r_ready")
        s_g2 = sem("gram_copied")
        s_rb = sem("emb_r_ready")
        s_zc = sem("z_copied")
        s_rz = sem("z_r_ready")
        s_h1r = sem("h1_relu")
        s_h2r = sem("h2_relu")
        s_yc = sem("y_copied")
        s_chain = sem("prep_chain")
        s_gmr = sem("emb_product_ready")
        s_vb = sem("emb_var_part")
        s_vbe = sem("emb_var_eps")
        s_vbr = sem("emb_var_reciprocal")
        s_sc = sem("emb_scaled")
        s_c = sem("centred_ready")
        s_v2 = sem("feature_var")
        s_v2e = sem("feature_var_eps")
        s_r2 = sem("feature_r2")
        s_m = sem("moving_ready")
        s_za = sem("z_squares_added")
        s_zv = sem("z_var_eps")
        s_zr = sem("z_var_reciprocal")
        s_zd = sem("z_r_diagonal")
        s_zs = sem("z_scaled")

        def unit(H, k):
            return not isinstance(H, int) or 0 <= UPP * H + k < NUNIT

        def split(H, k, S):
            if S is None:
                return isinstance(H, int) and (H, k) == (2, 8)
            return k not in WHOLE

        def split_count(k, S):
            n = sum(u not in WHOLE for u in range(8, k + 1))
            return n if S is None else S * SPLITS + n

        def super_of(x, S):
            return x[:, :, bass.ds(S * GPS, GPS)]

        x_banks = [ps_y[:, 0, :], ps_y[:, 1, :], ps_ab[0][:], ps_ab[1][:]]
        wl_banks = [ps_q[:, 0:NPAIR // 2], ps_rf[:, 0:NPAIR // 2]]
        r_banks = [ps_y[:, 0, :], ps_y[:, 1, :], ps_q[:], ps_rf[:]]

        def gram_rows(queue, S, j):
            g0 = (S * GPS) % (2 * GPS)
            rows = gram_d[S][0:SX_D].rearrange("(q p) j g -> p q j g", q=QN)
            for q0, nq, p0, np_ in WRITTEN:
                queue.dma_start(
                    rows[p0:p0 + np_, q0:q0 + nq, j, :],
                    gram[PROJ * j + p0:PROJ * j + p0 + np_, q0:q0 + nq, bass.ds(g0, GPS)],
                ).then_inc(s_fw, 16)

        z_banks = [ps_ab[0][:], ps_ab[1][:], ps_ab[0][:], ps_ab[1][:]]
        h1_banks = [ps_ab[1][:], ps_ab[0][:], ps_ab[1][:], ps_ab[0][:]]
        last_z_banks = [ps_ab[0][:], ps_ab[1][:], ps_gm[:], ps_rf[:]]
        last_h1_banks = [ps_y[:, 0, :], ps_y[:, 1, :], ps_q[:], ps_tr[:]]

        def is_last(S):
            return isinstance(S, int) and S == NSUPER - 1

        block = ctx.enter_context(nc.Block())

        @block.sync
        def _(sp):
            def load(dst, src, name):
                sp.dma_start(dst, src).then_inc(s_ld[name], 16)

            def write_scaled(tile, parity):
                sp.wait_ge(s_sc, tile + 1)
                rows = scaled_d[tile].rearrange("(b n) d -> b (n d)", n=NTAB)
                for h in range(2):
                    b = slice(h * TILE // 2, (h + 1) * TILE // 2)
                    sp.dma_start(rows[b], emb[parity][b]).then_inc(s_sw[parity][h], 16)

            def load_unit(tile, parity, nth, u, first=False):
                if u == 0:
                    sp.wait_ge(s_sw[parity][0], 16 * nth)
                if not first:
                    sp.wait_ge(s_q, tile * UPT + (u - UPT + 1))
                if u == 2:
                    sp.wait_ge(s_sw[parity][1], 16 * nth)
                src = scaled_d[tile][u * GPU * GROWS:(u + 1) * GPU * GROWS, :].rearrange(
                    "(g r) d -> r g d", r=GROWS)
                sp.dma_start(xe[u][:].rearrange("r (g d) -> r g d", g=GPU), src).then_inc(s_xl[u], 16)

            def write_gram(S):
                sp.wait_ge(s_g2, UPS * S + UPS)
                for j in range(BPG):
                    gram_rows(sp, S, j)

            def read_gram(S):
                if not isinstance(S, int) or S > 0:
                    sp.wait_ge(s_z, 4 * S)
                sp.wait_ge(s_fw, 16 * WRITES * (S + 1))
                rows = gram_d[S][0:SX_D].rearrange("(q p) j g -> q p (j g)", q=QN)
                for c, chunk in enumerate(CHUNKS):
                    row = 0
                    for q0, nq, p0, np_ in chunk:
                        if q0 < PROJ:
                            sp.dma_start(f_sb[row:row + nq * np_, c, :], rows[q0:q0 + nq, p0:p0 + np_, :]
                                         ).then_inc(s_fr, 16)
                        else:
                            sp.dma_start(f_sb[row:CH[c], c, :],
                                         gram_d[S][PROJ * PROJ:GRAM_ROWS].rearrange("r j g -> r (j g)")
                                         ).then_inc(s_fr, 16)
                        row += nq * np_

            def feed(H, c, S=None):
                tile, parity, nth = 2 * H + c, c % 2, H + (c // 2 + 1)
                write_scaled(tile, parity)
                for u in range(UPT - 1):
                    load_unit(tile, parity, nth, u)
                if S is not None:
                    write_gram(S)
                load_unit(tile, parity, nth, UPT - 1)
                if S is not None:
                    read_gram(S)

            sp.dma_start(ids[:], a["ids"].rearrange("(t p) n -> p t n", p=TILE)).then_inc(s_ids, 16)
            load(ws[:], a["L0_rec_Ws"], "ws")
            for n, v in enumerate(("gs", "bs", "gd", "bd")):
                load(vec[:, n:n + 1], a[f"L0_rec_{v}"].rearrange("(e o) -> e o", o=1), "vec")
            load(wsi[:], a["L0_rec_Wsi"], "wsi")
            load(wd, a["L0_rec_Wd"], "wd")
            load(gsi_row[:, 0:PROJ], a["L0_rec_gsi"].rearrange("(o p) -> o p", o=1), "gsi")
            load(gsi_row[:, PROJ:], a["L0_rec_bsi"].rearrange("(o p) -> o p", o=1), "gsi")
            load(bl[:], a["L0_rec_bl"][0:USED].rearrange("(c o) -> o c", o=P), "bl")
            load(gl[:], a["L0_rec_gl"][0:USED].rearrange("(c o) -> o c", o=P), "gl")
            load(b1[:], a["b_top1"].rearrange("(c o) -> o c", o=P), "b1")
            load(b2[:], a["b_top2"].rearrange("(c o) -> o c", o=P), "b2")
            load(w3[:], a["W_top3"].rearrange("(c k) o -> k (c o)", k=P), "w3")

            write_scaled(0, 0)
            for u in range(UPT):
                load_unit(0, 0, 1, u, first=True)
            feed(0, 1)
            sp.wait_ge(s_a["sx"], NSUPER)
            for s in range(NSUPER):
                sp.dma_start(gram_d[s][SX_D:GRAM_ROWS].rearrange("r j g -> r (j g)"), f_sb[0:1, s, :]).then_inc(s_sxw, 16)
            with sp.Fori(0, 2) as H:
                feed(H, 2)
                feed(H, 3)
            write_gram(0)
            sp.wait_ge(s_sxw, 16 * NSUPER)
            read_gram(0)
            feed(2, 2)
            with sp.Fori(0, 2) as T:
                feed(2 * T + 2, 3)
                feed(2 * T + 2, 4)
                feed(2 * T + 2, 5, S=T + 1)
                feed(2 * T + 2, 6)
            feed(6, 3)
            write_gram(NSUPER - 1)
            read_gram(NSUPER - 1)

        @block.gpsimd
        def _(pool):
            nc.gpsimd.memset(ident[:], 0.0).then_inc(s_const, 1)
            nc.gpsimd.memset(group_mask[:], 1.0).then_inc(s_const, 1)
            nc.gpsimd.memset(ones[:], 1.0).then_inc(s_const, 1)
            nc.gpsimd.memset(mean_e[:], 1.0 / E_DIM).then_inc(s_const, 1)
            nc.gpsimd.memset(mean_o[:], 1.0 / MAXD).then_inc(s_const, 1)
            nc.gpsimd.memset(mean_p[:], 1.0 / PROJ).then_inc(s_const, 1)
            nc.gpsimd.memset(gbd[:], 0.0).then_inc(s_const, 1)
            nc.gpsimd.memset(wp[0][:], 0.0).then_inc(s_const, 1)
            nc.gpsimd.memset(wp[1][:], 0.0).then_inc(s_const, 1)
            pool.wait_ge(s_const, 9)
            nc.gpsimd.affine_select(out=ident[:], in_=ident[:], compare_op=ALU.not_equal, fill=1.0, base=0,
                                    pattern=[[-1, P]], channel_multiplier=1).then_inc(s_const, 1)
            nc.gpsimd.affine_select(out=group_mask[:], in_=group_mask[:], compare_op=ALU.is_ge, fill=0.0, base=0,
                                    pattern=[[-NTAB, BPG]], channel_multiplier=1).then_inc(s_const, 1)
            pool.wait_ge(s_const, 11)
            nc.gpsimd.affine_select(out=group_mask[:], in_=group_mask[:], compare_op=ALU.is_ge, fill=0.0,
                                    base=NTAB - 1, pattern=[[NTAB, BPG]], channel_multiplier=-1
                                    ).then_inc(s_const, 1)

            def gather(tile, parity, earlier):
                if not isinstance(earlier, int) or earlier > 0:
                    for h in range(2):
                        pool.wait_ge(s_sw[parity][h], 16 * earlier)
                nc.gpsimd.tensor_copy(idx[parity][:], ids[:, tile, :]).then_inc(s_idx, 1)
                pool.wait_ge(s_idx, tile + 1)
                pool.sem_inc(s_begun, 1)
                for u in range(4):
                    for n in range(TAB0[u], TAB0[u + 1]):
                        nc.gpsimd.indirect_dma_start(
                            emb[parity][:, n * D:(n + 1) * D], None, tables[n],
                            bass.IndirectOffsetOnAxis(ap=idx[parity][:, n:n + 1], axis=0),
                        ).then_inc(s_gat[parity][u], 16)

            pool.wait_ge(s_ids, 16)
            gather(0, 0, 0)
            gather(1, 1, 0)
            with pool.Fori(1, NTILE // 2) as h:
                gather(2 * h, 0, h)
                gather(2 * h + 1, 1, h)

        @block.tensor
        def _(pe):
            mm, tr = nc.tensor.matmul, nc.tensor.transpose

            pe.wait_ge(s_const, 12)
            pe.wait_ge(s_ld["ws"], 16)
            mm(ps_ab[0][:, 0:D], mean_e[:], ws[:], start=True, stop=True).then_inc(s_p["wsmean"], 1)
            pe.wait_ge(s_ld["wsi"], 16)
            mm(ps_ab[1][0:PROJ, 0:NTAB], mean_p[:], wsi[:], start=True, stop=True).then_inc(s_p["wsimean"], 1)
            pe.wait_ge(s_ld["wd"], 16)
            mm(ps_y[:, 0, 0:D_DENSE], mean_e[:], wd, start=True, stop=True).then_inc(s_p["wdmean"], 1)
            pe.wait_ge(s_v["wc"], 1)
            mm(ps_ab[0][:, 0:2 * D], wc2, wc2, start=True, stop=True).then_inc(s_p["g"], 1)
            pe.wait_ge(s_v["wsi"], 1)
            tr(ps_ab[1][0:GROWS, 0:PROJ], wsc[:].rearrange("p j n -> p (j n)"),
               ident[0:PROJ, 0:PROJ]).then_inc(s_p["wsit"], 1)
            pe.wait_ge(s_v["wd"], 1)
            for k in range(2):
                last = tr(ps_y[:, 1, k * P:(k + 1) * P], wd[:, k * P:(k + 1) * P], ident[:])
            last.then_inc(s_p["wdt"], 1)
            pe.wait_ge(s_v["g"], 1)
            tr(ps_ab[0][:, 0:P], wg2, ident[:]).then_inc(s_p["wpt"], 1)
            pe.wait_ge(s_v["wsct"], 1)
            mm(ps_ab[1][:, 0:PROJ], ones[0:NTAB, :], wsct[0:NTAB, :], start=True, stop=True
               ).then_inc(s_p["sc"], 1)
            pe.wait_ge(s_v["bias"], 1)
            tr(ps_ab[1][0:PROJ, 0:P], bias_y[:], ident[:]).then_inc(s_p["biast"], 1)
            pe.wait_ge(s_ld["gsi"], 32)
            pe.wait_ge(s_v["bias3"], 1)
            mm(ps_ab[1][:, 0:2 * PROJ], ones[0:1, :], gsi_row[:], start=True, stop=True).then_inc(s_p["gb"], 1)
            pe.wait_ge(s_ld["dense"], 16)
            for n in range(2 * NSUPER):
                kc, s = n % 2, n // 2
                if n >= 2:
                    pe.wait_ge(s_a["dense_t"], n - 1)
                bank = (ps_tr, ps_gm)[n % 2]
                for t in range(TPS):
                    last = tr(bank[:, t * P:(t + 1) * P], dense[:, TPS * s + t, kc * P:(kc + 1) * P], ident[:])
                last.then_inc(s_p["dense_t"], 1)

            def centred_x():
                pe.wait_ge(s_a["dense_t"], 2 * NSUPER)
                pe.wait_ge(s_a["wdt"], 1)
                pe.wait_ge(s_v["wp"], 1)
                pe.wait_ge(s_v["gb"], 1)
                for s in range(NSUPER):
                    for kc in range(2):
                        last = mm(x_banks[s], wdt[:, kc, :], super_of(dense_t[:, kc], s), start=(kc == 0), stop=(kc == 1))
                    last.then_inc(s_p["x"], 1)

            def wl_mean():
                pe.wait_ge(s_ld["wl"], 16)
                for h in range(2):
                    for c in range(4):
                        last = mm(wl_banks[h], mean_o[:], wl[:, c, h * (NPAIR // 2):(h + 1) * (NPAIR // 2)],
                                  start=(c == 0), stop=(c == 3))
                    last.then_inc(s_p["wlmean"], 1)

            def x_variance():
                pe.wait_ge(s_v["wlsub"], 1)
                for s in range(NSUPER):
                    pe.wait_ge(s_a["xsq"], s + 1)
                    for j in range(BPG):
                        last = mm(ps_rf[:, BPG * s + j:BPG * s + j + 1], x_sq[:, j, s * GPS:(s + 1) * GPS],
                                  mean_e[:, 0:1], start=True, stop=True)
                last.then_inc(s_p["xvar"], 1)

            def x_r_everywhere():
                pe.wait_ge(s_v["xdiag"], 1)
                for s in range(NSUPER):
                    mm(r_banks[s], ones[:], x_diag[:, BPG * s:BPG * (s + 1), :].rearrange("p n b -> p (n b)"),
                       start=True, stop=True).then_inc(s_p["xbc"], 1)

            def sum_of_x(s):
                pe.wait_ge(s_a["x"], 1)
                if s >= 1:
                    pe.wait_ge(s_a["sx"], s)
                mm(ps_ab[0][0:1, :], ones[:, 0:1], super_of(xt[:], s), start=True, stop=True).then_inc(s_p["sx"], 1)

            def front_transpose(H, k):
                f = k + LEAD
                par, u = (f // UPT) % 2, f % UPT
                pe.wait_ge(s_gat[par][u], 16 * (TAB0[u + 1] - TAB0[u]) * (H + (f // UPP + 1)))
                if f > 0:
                    pe.wait_ge(s_et, UPP * H + f)
                for m in range(PAIRS[u]):
                    c0 = (TAB0[u] + 2 * m) * D
                    last = tr(ps_tr[:, m * P:(m + 1) * P], emb[par][:, c0:c0 + P], ident[:])
                last.then_inc(s_tr, 1)

            def front_g(H, k):
                f = k + LEAD
                pe.wait_ge(s_et, UPP * H + (f + 1))
                if f > 0:
                    pe.wait_ge(s_gmr, UPP * H + f)
                for m in range(PAIRS[f % UPT]):
                    last = mm(ps_gm[:, m * P:(m + 1) * P], emb_t[f % 2][:, m * P:(m + 1) * P], gbd[:],
                              start=True, stop=True)
                last.then_inc(s_gm, 1)

            def over_tables(H, k, S=None):
                u = k % UPT
                pe.wait_ge(s_xl[u], 32 * H + 16 * (k // UPT + 1))
                if split(H, k - 1, S):
                    pe.wait_ge(s_ql, split_count(k - 1, S))
                elif k >= 1:
                    pe.wait_ge(s_qt, UPP * H + k)
                for g in range(4):
                    last = mm(ps_q[:, g * P:(g + 1) * P], xe[u][:, g * P:(g + 1) * P],
                              wbd[:].rearrange("r j p -> r (j p)"), start=True, stop=True)
                last.then_inc(s_q, 1)

            def features(H, k, S=None):
                if k >= 1:
                    pe.wait_ge(s_sq, UPP * H + k)
                for a_ in range(2):
                    mm(ps_y[:, a_, :], bias_t[:], select[:].rearrange("k b p -> k (b p)"), start=True, stop=False)
                if split(H, k, S):
                    pe.wait_ge(s_ql, split_count(k, S))
                    for a_ in range(2):
                        mm(ps_y[:, a_, :], w_high[:], qs[k % 2][:, a_, :], start=False, stop=False)
                        last = mm(ps_y[:, a_, :], w_low[:], qs[k % 2][:, a_, :], start=False, stop=True)
                else:
                    pe.wait_ge(s_qt, UPP * H + (k + 1))
                    for a_ in range(2):
                        last = mm(ps_y[:, a_, :], wp[a_][:], qt[k % 2][:], start=False, stop=True)
                last.then_inc(s_y, 1)

            def gram_product(H, k):
                pe.wait_ge(s_m, UPP * H + (k + 1))
                if k >= 1:
                    pe.wait_ge(s_g2, UPP * H + k)
                for a_ in range(2):
                    for g in range(4):
                        for j in range(BPG):
                            last = mm(ps_r[PROJ * j:PROJ * (j + 1), 2 * g + a_, :], cen[k % 2][:, a_, g, j, :],
                                      mov[k % 2][:, a_, g, j, :], start=True, stop=True,
                                      tile_position=(0, PROJ * j))
                last.then_inc(s_gr, 1)

            def step(H, k, S=None):
                if S is not None:
                    tail_early(S, k - 8)
                if unit(H, k + LEAD):
                    front_transpose(H, k)
                if unit(H, k + 1) and not split(H, k + 1, S):
                    over_tables(H, k + 1, S)
                if unit(H, k - 2):
                    gram_product(H, k - 2)
                if S is not None and k - 8 == 7:
                    square_sum(S)
                if unit(H, k + 1) and split(H, k + 1, S):
                    over_tables(H, k + 1, S)
                if unit(H, k + LEAD):
                    front_g(H, k)
                if unit(H, k):
                    features(H, k, S)
                if S is not None:
                    tail(S, k - 8)

            def outputs(S, products):
                for i in products:
                    c, n = i // NCHUNK, i % NCHUNK
                    if i == 0:
                        pe.wait_ge(s_fr, 16 * READS * (S + 1))
                        pe.wait_ge(s_yc, S + 1)
                    if n == 0 and c >= 2 and not is_last(S):
                        pe.wait_ge(s_zc, 4 * S + (c - 1))
                    last = mm((last_z_banks if is_last(S) else z_banks)[c], wl_t[0:CH[n], n, c * P:(c + 1) * P], f_sb[0:CH[n], n, :],
                              start=(n == 0), stop=(n == NCHUNK - 1))
                    if n == NCHUNK - 1:
                        last.then_inc(s_z, 1)

            def square_sum(S):
                pe.wait_ge(s_za, 3 * S + 3)
                for j in range(BPG):
                    last = mm(ps_ab[0][:, j:j + 1], z_sq[:, 0, j * GPS:(j + 1) * GPS], mean_o[:, 0:1],
                              start=True, stop=True)
                last.then_inc(s_ss, 1)

            def r_everywhere(S):
                pe.wait_ge(s_zd, S + 1)
                mm(ps_ab[0][:], ones[:], z_diag.rearrange("p n b -> p (n b)"), start=True, stop=True).then_inc(s_zb, 1)

            def layer1_dense(S, h):
                if is_last(S):
                    pe.wait_ge(*((s_sq, NUNIT), (s_sq, NUNIT), (s_qt, NUNIT), (s_et, NUNIT))[h])
                elif h == 0:
                    pe.wait_ge(s_zc, 4 * S + 4)
                elif h == 1:
                    pe.wait_ge(s_zs, S + 1)
                elif h >= 2:
                    pe.wait_ge(s_h1r, 4 * S + (h - 1))
                for kc in range(2):
                    mm((last_h1_banks if is_last(S) else h1_banks)[h], w1[:, 3 + kc, h * P:(h + 1) * P], super_of(dense_t[:, kc], S),
                       start=(kc == 0), stop=False)

            def layer1_z(S, h, kcs=range(3)):
                if h == 0:
                    pe.wait_ge(s_zs, S + 1)
                for kc in kcs:
                    last = mm((last_h1_banks if is_last(S) else h1_banks)[h], w1[:, kc, h * P:(h + 1) * P], z_sb[:, kc, :],
                              start=False, stop=(kc == 2))
                if kcs[-1] == 2:
                    last.then_inc(s_h1, 1)

            def layer2(S, h, kcs):
                for kc in kcs:
                    if h == 0 or kc == 0:
                        pe.wait_ge(s_h1r, 4 * S + max(kc + 1, h + 3))
                    last = mm(ps_ab[1 - h][:], w2[:, kc, h * P:(h + 1) * P], h1_sb[:, kc, :],
                              start=(kc == 0), stop=(kc == 3))
                if kcs[-1] == 3:
                    last.then_inc(s_h2, 1)

            def layer3(S):
                for kc in range(2):
                    pe.wait_ge(s_h2r, 2 * S + (kc + 1))
                    last = mm(ps_ab[1][0:1, :], w3[:, kc:kc + 1], h2_sb[:, kc, :], start=(kc == 0), stop=(kc == 1))
                last.then_inc(s_yo, 1)

            def tail(S, part):
                if part < 6:
                    outputs(S, range(*((0, 4, 8, 12, 15, 18, 20)[part:part + 2])))
                elif part == 6:
                    layer1_dense(S, 0)
                elif part == 9:
                    layer1_z(S, 0)
                elif part == 10:
                    layer1_dense(S, 1)
                    layer1_z(S, 1, range(0, 2))
                elif part == 11:
                    layer1_z(S, 1, range(2, 3))
                    layer1_dense(S, 2)
                    layer1_z(S, 2, range(0, 1))
                elif part == 12:
                    layer1_z(S, 2, range(1, 3))
                    layer1_dense(S, 3)
                elif part == 13:
                    layer1_z(S, 3)
                    layer2(S, 0, range(0, 1))
                elif part == 14:
                    layer2(S, 0, range(1, 4))
                    layer2(S, 1, range(0, 1))
                elif part == 15:
                    layer3(S)

            def tail_early(S, part):
                if part == 8:
                    r_everywhere(S)
                elif part == 15:
                    layer2(S, 1, range(1, 4))

            def weight_transpose(n):
                if n >= 1 and n < 4:
                    pe.wait_ge(s_a["wlt"], n + 1)
                for c in range(4):
                    last = tr(ps_ab[(0, 1, 0, 1, 1)[n]][0:CH[n], c * P:(c + 1) * P],
                              wl_x[:, c, ROW0[n]:ROW0[n] + CH[n]], ident[:])
                last.then_inc(s_p["wlt"], 1)

            def bl_through_layer1():
                pe.wait_ge(s_v["xc"], NSUPER)
                pe.wait_ge(s_ld["w1"], 32)
                pe.wait_ge(s_ld["bl"], 16)
                for h in range(4):
                    for kc in range(3):
                        last = mm(ps_ab[1][:, h:h + 1], w1[:, kc, h * P:(h + 1) * P], bl[:, kc:kc + 1],
                                  start=(kc == 0), stop=(kc == 2))
                last.then_inc(s_p["b1"], 1)

            pe.wait_ge(s_a["dense_t"], 2 * NSUPER)
            for k in range(-LEAD, 0):
                front_transpose(0, k)
                front_g(0, k)
                if k == -6:
                    centred_x()
                elif k == -5:
                    wl_mean()
                elif k == -4:
                    x_variance()
                elif k == -3:
                    x_r_everywhere()
            pe.wait_ge(s_v["x"], 1)
            over_tables(0, 0)
            for k in range(4):
                step(0, k)
                sum_of_x(k)
                if k == 2:
                    bl_through_layer1()
            pe.wait_ge(s_ld["w2"], 16)
            pe.wait_ge(s_v["b1"], 1)
            with pe.Fori(0, 2) as H:
                for k in range(4, 12):
                    step(H, k)
            pe.wait_ge(s_v["wlrows"], 4)
            for k in range(4, 8):
                weight_transpose(k - 4)
                if k == 4:
                    weight_transpose(4)
                step(2, k)
            pe.wait_ge(s_a["wlt"], NCHUNK)
            pe.wait_ge(s_ld["w3"], 16)
            with pe.Fori(0, 2) as T:
                for k in range(8, 24):
                    step(2 * T + 2, k, T)
            for k in range(8, 24):
                step(6, k, 2)
            S = NSUPER - 1
            pe.wait_ge(s_gmr, NUNIT)
            pe.wait_ge(s_g2, NUNIT)
            outputs(S, range(4 * NCHUNK))
            layer1_dense(S, 0)
            layer1_dense(S, 1)
            square_sum(S)
            layer1_dense(S, 2)
            layer1_dense(S, 3)
            r_everywhere(S)
            for h in range(4):
                layer1_z(S, h)
            for h in range(2):
                layer2(S, h, range(4))
            layer3(S)

        @block.scalar
        def _(act):
            cp = nc.scalar.copy

            act.wait_ge(s_ld["ws"], 16)
            act.dma_start(dense, a["r_dense_t"].rearrange("(t p) k -> p t k", p=TILE)).then_inc(s_ld["dense"], 16)
            act.wait_ge(s_p["wdt"], 1)
            cp(wdt[:].rearrange("p k e -> p (k e)"), ps_y[:, 1, 0:2 * P]).then_inc(s_a["wdt"], 1)
            act.wait_ge(s_ld["dense"], 16)
            act.dma_start(wl[:], a["L0_rec_Wl"].rearrange("(c o) k -> o c k", o=P)).then_inc(s_ld["wl"], 16)
            for n in range(2 * NSUPER):
                kc, s = n % 2, n // 2
                act.wait_ge(s_p["dense_t"], n + 1)
                cp(super_of(dense_t[:, kc], s).rearrange("k j g -> k g j"),
                   (ps_tr, ps_gm)[n % 2][:].rearrange("k (g j) -> k g j", j=BPG)).then_inc(s_a["dense_t"], 1)
            def sum_of_x(s):
                act.wait_ge(s_p["sx"], s + 1)
                cp(f_sb[0:1, s, :], ps_ab[0][0:1, :]).then_inc(s_a["sx"], 1)

            def front_copy(H, k):
                f = k + LEAD
                w = PAIRS[f % UPT] * P
                act.wait_ge(s_tr, UPP * H + (f + 1))
                if f >= 2:
                    act.wait_ge(s_gm, UPP * H + (f - 1))
                cp(emb_t[f % 2][:, 0:w], ps_tr[:, 0:w]).then_inc(s_et, 1)

            def front_sqrt(H, k):
                f = k + LEAD
                if f % UPT == UPT - 1:
                    act.wait_ge(s_vbr, 2 * H + (f // UPT + 1))
                    nc.scalar.activation(rs_b[:], var_r[:], ACT.Sqrt).then_inc(s_rb, 1)

            def q_copy(H, k, S=None):
                act.wait_ge(s_q, UPP * H + (k + 1))
                if k >= 2:
                    act.wait_ge(s_y, UPP * H + (k - 1))
                if split(H, k, S):
                    cp(qs[k % 2][0:D, 0, :], ps_q[0:D, :])
                    cp(qs[k % 2][D:P, 1, :], ps_q[D:P, :]).then_inc(s_qt, 1)
                else:
                    cp(qt[k % 2][:], ps_q[:]).then_inc(s_qt, 1)

            def feature_copy(H, k):
                act.wait_ge(s_y, UPP * H + (k + 1))
                if k >= 2:
                    act.wait_ge(s_gr, UPP * H + (k - 1))
                both = ps_y[:].rearrange("e a (g j p) -> e a g j p", j=BPG, p=PROJ)
                cp(cen[k % 2][:], both).then_inc(s_c, 1)
                if k >= 1:
                    act.wait_ge(s_v2, UPP * H + k)
                nc.scalar.activation(sq[:], both, ACT.Square).then_inc(s_sq, 1)

            def feature_sqrt(H, k):
                act.wait_ge(s_r2, UPP * H + (k + 1))
                nc.scalar.activation(mov[k % 2][:, :, :, :, QN - 1], r2[:], ACT.Sqrt).then_inc(s_rs, 1)

            def gram_copy(H, k, written=None):
                act.wait_ge(s_gr, UPP * H + (k + 1))
                if written is not None:
                    act.wait_ge(s_fw, 16 * WRITES * written)
                g0 = (H * (UPP * GPU) + k * GPU) % (2 * GPS)
                cp(gram[:, :, bass.ds(g0, GPU)], ps_r.rearrange("p g q -> p q g")).then_inc(s_g2, 1)

            def step(H, k, written=None, S=None):
                if unit(H, k - 1) and (k >= 1):
                    feature_copy(H, k - 1)
                if unit(H, k + LEAD):
                    front_copy(H, k)
                if S is not None and unit(H, k - 1):
                    feature_sqrt(H, k - 1)
                if unit(H, k + 1):
                    q_copy(H, k + 1, S)
                if S is not None:
                    tail(S, k - 8)
                if unit(H, k - 2) and k >= 2:
                    gram_copy(H, k - 2, written)
                if S is None and unit(H, k - 1) and k >= 1:
                    feature_sqrt(H, k - 1)
                if unit(H, k + LEAD):
                    front_sqrt(H, k)
                if S is not None:
                    tail_late(S, k - 8)

            def z_copy(S, c):
                bank = (last_z_banks if is_last(S) else z_banks)[c]
                act.wait_ge(s_z, 4 * S + (c + 1))
                if c < 3:
                    nc.scalar.activation(z_c[:, c, :], bank, ACT.Identity, bias=const_z[:, c:c + 1])
                nc.scalar.activation(z_sq[:, c, :], bank, ACT.Square,
                                     bias=const_z[:, c:c + 1]).then_inc(s_zc, 1)

            def h1_relu(S, h):
                act.wait_ge(s_h1, 4 * S + (h + 1))
                nc.scalar.activation(h1_sb[:, h, :], (last_h1_banks if is_last(S) else h1_banks)[h], ACT.Relu,
                                     bias=b1x[:, h:h + 1]).then_inc(s_h1r, 1)

            def h2_relu(S, h):
                act.wait_ge(s_h2, 2 * S + (h + 1))
                nc.scalar.activation(h2_sb[:, h, :], ps_ab[1 - h][:], ACT.Relu,
                                     bias=b2[:, h:h + 1]).then_inc(s_h2r, 1)

            def tail(S, part):
                if part in (2, 3, 4, 6):
                    z_copy(S, (2, 3, 4, 6).index(part))
                elif part == 10:
                    h1_relu(S, 0)
                elif 12 <= part < 15:
                    h1_relu(S, part - 11)
                elif part == 15:
                    h2_relu(S, 0)

            def tail_late(S, part):
                if part == 7:
                    act.wait_ge(s_zr, S + 1)
                    nc.scalar.activation(rt_s[:, 0:TPS], rec_s[:, 0:TPS], ACT.Sqrt).then_inc(s_rz, 1)
                elif part == 15:
                    h2_relu(S, 1)

            def output(S):
                act.wait_ge(s_yo, S + 1)
                act.wait_ge(s_out, 16 * (S + 1))
                cp(y_sb[:].rearrange("o (g j) -> o g j", j=BPG),
                   ps_ab[1][0:1, :].rearrange("o (j g) -> o g j", j=BPG)).then_inc(s_yc, 1)
                act.wait_ge(s_yc, S + 2)
                act.dma_start(out[bass.ds(S * SUPER, SUPER), :].rearrange("(o b) c -> o (b c)", o=1), y_sb[:]
                              ).then_inc(s_out, 16)

            front_copy(0, -LEAD)
            act.dma_start(w1[:, 0:3, :], a["W_top1"][0:USED, :].rearrange("(c k) h -> k c h", k=P)
                          ).then_inc(s_ld["w1"], 16)
            act.dma_start(w1[:, 3:5, :], a["W_top1"][MAXD:, :].rearrange("(c k) h -> k c h", k=P)
                          ).then_inc(s_ld["w1"], 16)
            act.dma_start(w2[:], a["W_top2"].rearrange("(c k) h -> k c h", k=P)).then_inc(s_ld["w2"], 16)
            for s in range(NSUPER):
                act.wait_ge(s_v["xc"], s + 1)
                nc.scalar.activation(super_of(x_sq, s), super_of(xt[:], s), ACT.Square).then_inc(s_a["xsq"], 1)
            for k in range(-LEAD + 1, 0):
                front_copy(0, k)
                if k == -4:
                    act.wait_ge(s_v["xrr"], 1)
                    nc.scalar.activation(rt_s[:], rec_s[:], ACT.Sqrt).then_inc(s_a["xrt"], 1)
                front_sqrt(0, k)
                if k == -3:
                    act.wait_ge(s_v["x"], 1)
                    nc.scalar.activation(xt[:], xt[:], ACT.Identity, bias=vec[:, 3:4]).then_inc(s_a["x"], 1)
            q_copy(0, 0)
            for k in range(4):
                step(0, k)
                sum_of_x(k)
            with act.Fori(0, 2) as H:
                for k in range(4, 12):
                    step(H, k)

            def weight_copy(n, nth):
                act.wait_ge(s_p["wlt"], nth)
                cp(wl_t[0:CH[n], n, :], ps_ab[(0, 1, 0, 1, 1)[n]][0:CH[n], :]).then_inc(s_a["wlt"], 1)

            for k in range(4, 8):
                step(2, k)
                weight_copy(k - 4, k - 3 if k == 4 else k - 2)
                if k == 4:
                    weight_copy(4, 2)
            act.wait_ge(s_ld["b2"], 16)
            act.wait_ge(s_v["b1"], 1)
            act.sem_inc(s_out, 16)
            act.sem_inc(s_yc, 1)
            with act.Fori(0, 2) as T:
                for k in range(8, 24):
                    step(2 * T + 2, k, T + 1 if k == 18 else None, T)
                output(T)
            for k in range(8, 24):
                step(6, k, None, 2)
            output(2)
            for part in range(16):
                tail(3, part)
                tail_late(3, part)
            output(3)
            act.wait_ge(s_out, 16 * (NSUPER + 1))

        @block.vector
        def _(dve):
            tt, ts = nc.vector.tensor_tensor, nc.vector.tensor_scalar
            chain = [0]

            def link(ins):
                chain[0] += 1
                ins.then_inc(s_chain, 1)
                dve.wait_ge(s_chain, chain[0])

            nc.vector.memset(wl_low[:], 0.0).then_inc(s_v["low"], 1)
            dve.wait_ge(s_p["wsmean"], 1)
            for h in range(2):
                last = tt(wc2[:, h * D:(h + 1) * D], ws[:], ps_ab[0][:, 0:D], ALU.subtract)
            last.then_inc(s_v["wc"], 1)
            dve.wait_ge(s_p["wsimean"], 1)
            for j in range(BPG):
                last = tt(wsc[:, j, :], wsi[:], ps_ab[1][0:PROJ, 0:NTAB], ALU.subtract)
            last.then_inc(s_v["wsi"], 1)
            dve.wait_ge(s_p["wdmean"], 1)
            tt(wd, wd, ps_y[:, 0, 0:D_DENSE], ALU.subtract).then_inc(s_v["wd"], 1)
            dve.wait_ge(s_p["g"], 1)
            dve.wait_ge(s_const, 12)
            dve.wait_ge(s_ld["vec"], 64)
            dve.wait_ge(s_v["wc"], 1)
            for h in range(2):
                r = slice(h * D, (h + 1) * D)
                ts(gbd[r, r], ps_ab[0][r, r], 1.0 / E_DIM, None, ALU.mult)
            ts(wg2, wc2, vec[:, 0:1], None, ALU.mult).then_inc(s_v["g"], 1)
            dve.wait_ge(s_p["wsit"], 1)
            nc.vector.tensor_copy(wsct[:], ps_ab[1][0:GROWS, 0:PROJ]).then_inc(s_v["wsct"], 1)
            dve.wait_ge(s_v["wsct"], 1)
            for j in range(BPG):
                last = ts(wbd[:, j, :], wsct[:], group_mask[:, j:j + 1], None, ALU.mult)
            last.then_inc(s_v["wbd"], 1)
            dve.wait_ge(s_p["wpt"], 1)
            nc.vector.tensor_copy(wp[0][0:D, :], ps_ab[0][0:D, 0:P])
            nc.vector.tensor_copy(wp[1][D:2 * D, :], ps_ab[0][D:2 * D, 0:P])
            link(nc.vector.tensor_copy(w_high[:], ps_ab[0][:, 0:P]))
            tt(w_low[:], ps_ab[0][:, 0:P], w_high[:], ALU.subtract).then_inc(s_v["wp"], 1)
            dve.wait_ge(s_p["sc"], 1)
            ts(bias_y[:], ps_ab[1][:, 0:PROJ], vec[:, 1:2], None, ALU.mult).then_inc(s_v["bias"], 1)
            for q in range(3):
                r = slice(q * PROJ, (q + 1) * PROJ)
                nc.vector.tensor_copy(select[r], ident[r, r].unsqueeze(1).to_broadcast([PROJ, 512 // PROJ, PROJ]))
            dve.wait_ge(s_p["biast"], 1)
            link(nc.vector.tensor_copy(bias_h[:], ps_ab[1][0:PROJ, 0:P]))
            nc.vector.tensor_copy(bias_t[0:PROJ, :], bias_h[:])
            link(tt(bias_r[:, 0, :], ps_ab[1][0:PROJ, 0:P], bias_h[:], ALU.subtract))
            link(nc.vector.tensor_copy(bias_h[:], bias_r[:, 0, :]))
            nc.vector.tensor_copy(bias_t[PROJ:2 * PROJ, :], bias_h[:])
            link(tt(bias_r[:, 1, :], bias_r[:, 0, :], bias_h[:], ALU.subtract))
            nc.vector.tensor_copy(bias_t[2 * PROJ:3 * PROJ, :], bias_r[:, 1, :]).then_inc(s_v["bias3"], 1)
            dve.wait_ge(s_p["gb"], 1)
            nc.vector.tensor_copy(gb[:], ps_ab[1][:, 0:2 * PROJ]).then_inc(s_v["gb"], 1)

            def centred_x():
                for s in range(NSUPER):
                    dve.wait_ge(s_p["x"], s + 1)
                    nc.vector.tensor_copy(super_of(xt[:], s), x_banks[s].rearrange("e (j g) -> e j g", j=BPG)
                                          ).then_inc(s_v["xc"], 1)

            def wl_centred():
                for h in range(2):
                    dve.wait_ge(s_p["wlmean"], h + 1)
                    for c in range(4):
                        r = slice(h * (NPAIR // 2), (h + 1) * (NPAIR // 2))
                        last = tt(wl[:, c, r], wl[:, c, r], wl_banks[h], ALU.subtract)
                last.then_inc(s_v["wlsub"], 1)

            def low_rows():
                dve.wait_ge(s_v["low"], 1)
                dve.wait_ge(s_v["wlsub"], 1)
                for p in range(PROJ):
                    r0 = p * (p + 1) // 2
                    last = nc.vector.tensor_copy(wl_low[:, :, 0:p + 1, p], wl[:, :, r0:r0 + p + 1])
                link(last)
                dve.wait_ge(s_v["gb"], 1)
                g_of = [P, PROJ, PROJ]
                link(tt(gg, gb[:, 0:PROJ].unsqueeze(1).to_broadcast(g_of),
                        gb[:, 0:PROJ].unsqueeze(2).to_broadcast(g_of), ALU.mult))

            def x_r():
                dve.wait_ge(s_p["xvar"], 1)
                ts(var_s[:], ps_rf[:, 0:NTILE], EPS, None, ALU.add).then_inc(s_v["xvar"], 1)
                dve.wait_ge(s_v["xvar"], 1)
                nc.vector.reciprocal(rec_s[:], var_s[:]).then_inc(s_v["xrr"], 1)

            def diagonals(out, r):
                return tt(out, ident[:].unsqueeze(1).to_broadcast(out.shape),
                          r.unsqueeze(2).to_broadcast(out.shape), ALU.mult)

            def x_diagonals():
                dve.wait_ge(s_a["xrt"], 1)
                diagonals(x_diag, rt_s[:]).then_inc(s_v["xdiag"], 1)

            def x_scale():
                for s in range(NSUPER):
                    dve.wait_ge(s_p["xbc"], s + 1)
                    last = nc.vector.scalar_tensor_tensor(
                        out=super_of(xt[:], s), in0=super_of(xt[:], s), scalar=vec[:, 2:3],
                        in1=r_banks[s].rearrange("e (j g) -> e j g", j=BPG), op0=ALU.mult, op1=ALU.mult)
                last.then_inc(s_v["x"], 1)

            def weight_rows(c, links, piece):
                at = bass.ds(c, 1)
                low_c = wl_low[:, at].rearrange("o c q p -> o (c q) p")
                wl_c = wl_x[:, at].rearrange("o c r -> o (c r)")
                cz = const_z[:, at]
                gsi, bsi = gb[:, 0:PROJ], gb[:, PROJ:]
                over_q = [P, PROJ + 1, PROJ]
                done = [(0, 2, 4, 9)[piece]]

                def link(ins):
                    done[0] += 1
                    ins.then_inc(s_chain, 1)
                    dve.wait_ge(s_chain, links + done[0])

                if piece == 0:
                    link(tt(prep_tmp[:], low_c, bsi.unsqueeze(1).to_broadcast(over_q), ALU.mult))
                    link(nc.vector.tensor_reduce(small[:, 0, :], prep_tmp[:], AX.X, ALU.add))
                elif piece == 1:
                    link(tt(prep_tmp[:, 0:PROJ, :], low_c[:, 1:, :],
                            bsi.unsqueeze(2).to_broadcast([P, PROJ, PROJ]), ALU.mult))
                    link(nc.vector.tensor_reduce(small[:, 1, 0:PROJ],
                                                 prep_tmp[:, 0:PROJ, :].rearrange("o q p -> o p q"), AX.X, ALU.add))
                elif piece == 2:
                    link(tt(small[:, 2, 0:PROJ], small[:, 0, 1:], bsi, ALU.mult))
                    link(nc.vector.tensor_reduce(cz, small[:, 2, 0:PROJ], AX.X, ALU.add))
                    link(ts(cz, cz, float(E_DIM), None, ALU.mult))
                    link(tt(small[:, 3, 0:PROJ], small[:, 0, 1:], small[:, 1, 0:PROJ], ALU.add))
                    link(tt(wl_c[:, XROW + PROJ:XROW + 2 * PROJ], small[:, 3, 0:PROJ], gsi, ALU.mult))
                    nc.vector.tensor_copy(wl_c[:, SXROW:NROW], small[:, 0, 0:1])
                else:
                    tt(wl_c[:, XROW:XROW + PROJ], low_c[:, 0, :], gsi, ALU.mult)
                    for row, q0, nq, p0, np_ in BLOCKS:
                        last = tt(wl_c[:, row:row + nq * np_].rearrange("o (q p) -> o q p", q=nq),
                                  low_c[:, 1 + q0:1 + q0 + nq, p0:p0 + np_],
                                  gg[:, q0:q0 + nq, p0:p0 + np_], ALU.mult)
                    last.then_inc(s_v["wlrows"], 1)

            def front_var(H, k):
                f = k + LEAD
                par, u = (f // UPT) % 2, f % UPT
                w = PAIRS[u] * P
                dve.wait_ge(s_gm, UPP * H + (f + 1))
                tt(prod[f % 2][:, 0:w], ps_gm[:, 0:w], emb[par][:, TAB0[u] * D:TAB0[u] * D + w], ALU.mult
                   ).then_inc(s_gmr, 1)
                dve.wait_ge(s_gmr, UPP * H + (f + 1))
                nc.vector.tensor_reduce(var_b[:, TAB0[u]:TAB0[u + 1]],
                                        prod[f % 2][:, 0:w].rearrange("b (n d) -> b n d", d=D), AX.X, ALU.add
                                        ).then_inc(s_vb, 1)

            def front_scale(H, k):
                f = k + LEAD
                if f % UPT == UPT - 1:
                    c = f // UPT
                    dve.wait_ge(s_vb, UPP * H + (f + 1))
                    ts(var_e[:], var_b[:], EPS, None, ALU.add).then_inc(s_vbe, 1)
                    dve.wait_ge(s_vbe, 2 * H + (c + 1))
                    nc.vector.reciprocal(var_r[:], var_e[:]).then_inc(s_vbr, 1)
                    dve.wait_ge(s_rb, 2 * H + (c + 1))
                    e = emb[c % 2][:].rearrange("b (n d) -> b n d", d=D)
                    tt(e, e, rs_b[:].unsqueeze(2).to_broadcast([P, NTAB, D]), ALU.mult).then_inc(s_sc, 1)

            def moving(H, k):
                p, n = k % 2, UPP * H + (k + 1)
                dve.wait_ge(s_sq, n)
                nc.vector.tensor_reduce(v2[:], sq[:].rearrange("e a g j p -> e (a g j) p"), AX.X, ALU.add
                                        ).then_inc(s_v2, 1)
                dve.wait_ge(s_v2, n)
                ts(v2e[:], v2[:], 1.0 / PROJ, EPS, ALU.mult, ALU.add).then_inc(s_v2e, 1)
                dve.wait_ge(s_v2e, n)
                nc.vector.reciprocal(r2[:].rearrange("e a g j -> e (a g j)"), v2e[:]).then_inc(s_r2, 1)
                dve.wait_ge(s_r2, n)
                m = mov[p][:].rearrange("e a g j q -> e (a g j) q")
                tt(m[:, :, 0:PROJ], cen[p][:].rearrange("e a g j p -> e (a g j) p"),
                   r2[:].rearrange("e a g j -> e (a g j)").unsqueeze(2).to_broadcast([P, UNIT, PROJ]), ALU.mult)
                dve.wait_ge(s_rs, n)
                x = xt[:, :, bass.ds(H * (UPP * GPU) + k * GPU, GPU)].rearrange("e j (g a) -> e a g j", a=2)
                for a_ in range(2):
                    last = tt(mov[p][:, a_, :, :, PROJ], mov[p][:, a_, :, :, PROJ + 1], x[:, a_], ALU.mult)
                last.then_inc(s_m, 1)

            def q_low(H, k):
                dve.wait_ge(s_qt, UPP * H + (k + 1))
                tt(qs[k % 2][D:P, 0, :], ps_q[0:D, :], qs[k % 2][0:D, 0, :], ALU.subtract)
                tt(qs[k % 2][0:D, 1, :], ps_q[D:P, :], qs[k % 2][D:P, 1, :], ALU.subtract).then_inc(s_ql, 1)

            def step(H, k, S=None):
                if unit(H, k - 1) and k >= 1:
                    moving(H, k - 1)
                if unit(H, k + LEAD):
                    front_var(H, k)
                if unit(H, k + 1) and split(H, k + 1, S):
                    q_low(H, k + 1)
                if unit(H, k + LEAD):
                    front_scale(H, k)
                for c, at in enumerate((12, 14, 14)):
                    if S is not None and k == at:
                        z_squares(S, c + 1)
                if S is not None and k == 15:
                    z_r(S)
                if S is not None and k == 16:
                    z_scale(S)

            def z_squares(S, c):
                dve.wait_ge(s_zc, 4 * S + (c + 1))
                if c >= 2:
                    dve.wait_ge(s_za, 3 * S + (c - 1))
                tt(z_sq[:, 0, :], z_sq[:, 0, :], z_sq[:, c, :], ALU.add).then_inc(s_za, 1)

            def z_r(S):
                dve.wait_ge(s_ss, S + 1)
                ts(var_s[:, 0:TPS], ps_ab[0][:, 0:TPS], EPS, None, ALU.add).then_inc(s_zv, 1)
                dve.wait_ge(s_zv, S + 1)
                nc.vector.reciprocal(rec_s[:, 0:TPS], var_s[:, 0:TPS]).then_inc(s_zr, 1)
                dve.wait_ge(s_rz, S + 1)
                diagonals(z_diag, rt_s[:, 0:TPS]).then_inc(s_zd, 1)

            def z_scale(S):
                dve.wait_ge(s_zb, S + 1)
                for c in range(3):
                    last = nc.vector.scalar_tensor_tensor(
                        out=z_sb[:, c, :], in0=z_c[:, c, :], scalar=gl[:, c:c + 1], in1=ps_ab[0][:],
                        op0=ALU.mult, op1=ALU.mult)
                last.then_inc(s_zs, 1)

            for k in range(-LEAD, 0):
                front_var(0, k)
                front_scale(0, k)
                if k == -6:
                    centred_x()
                elif k == -5:
                    wl_centred()
                elif k == -4:
                    x_r()
                elif k == -3:
                    x_diagonals()
                    low_rows()
                    x_scale()
                elif k >= -2:
                    weight_rows(0, chain[0], 2 * k + 4)
                    weight_rows(0, chain[0], 2 * k + 5)
            chain[0] += LINKS
            for k in range(4):
                step(0, k)
                weight_rows(1, chain[0], k)
            chain[0] += LINKS
            dve.wait_ge(s_p["b1"], 1)
            dve.wait_ge(s_ld["b1"], 16)
            tt(b1x[:], ps_ab[1][:, 0:4], b1[:], ALU.add).then_inc(s_v["b1"], 1)
            with dve.Fori(0, 2) as H:
                for k in range(4, 12):
                    step(H, k)
                    if k % 2 == 0:
                        weight_rows(H + 2, LINKS * H + chain[0], k // 2 - 2)
            dve.wait_ge(s_ld["gl"], 16)
            for k in range(4, 8):
                step(2, k)
            with dve.Fori(0, 2) as T:
                for k in range(8, 24):
                    step(2 * T + 2, k, T)
            for k in range(8, 24):
                step(6, k, 2)
            for c in range(1, 4):
                z_squares(3, c)
            z_r(3)
            z_scale(3)


_NAMES = (["r_dense_t", "ids"] + [f"tbl_{n}" for n in range(NTAB)]
          + ["W_top1", "b_top1", "W_top2", "b_top2", "W_top3"]
          + [f"L0_rec_{n}" for n in ("Wd", "gd", "bd", "Ws", "gs", "bs", "Wsi", "gsi", "bsi", "Wl", "gl", "bl")])


def kernel(**inputs):
    import numpy as np
    import concourse.bacc as bacc
    from concourse.bass_utils import run_bass_kernel_spmd

    nc = bacc.Bacc("TRN2", target_bir_lowering=False, num_devices=1)
    arrays, args = {}, {}
    for name in _NAMES:
        x = np.ascontiguousarray(inputs[name])
        arrays[f"in_{name}"] = x
        args[name] = nc.dram_tensor(f"in_{name}", x.shape, mybir.dt.from_np(x.dtype), kind="ExternalInput").ap()
    out = nc.dram_tensor("out_y", (ROWS, 1), F32, kind="ExternalOutput").ap()
    interaction_tower(nc, args, out)
    r = run_bass_kernel_spmd(nc, [arrays], core_ids=[0])
    return r.results[0]["out_y"]
```
